# Optimizing a Trainium2 kernel written in Bass

```python
import numpy as np
import jax
import jax.numpy as jnp

def _softmax(x, axis=-1):
    return jax.nn.softmax(x, axis=axis)

def _gelu(x):
    return jax.nn.gelu(x, approximate=True)

def _silu(x):
    return jax.nn.silu(x)

def _sigmoid(x):
    return jax.nn.sigmoid(x)

def _layernorm(x, axis=-1, eps=1e-05):
    m = jnp.mean(x, axis=axis, keepdims=True)
    v = jnp.var(x, axis=axis, keepdims=True)
    return (x - m) / jnp.sqrt(v + eps)

def _scatter_add(tgt, idx, src, axis=0):
    return tgt.at[idx].add(src)

def _segment_sum(src, seg, n):
    return jax.ops.segment_sum(src, seg, n)
kernel_name = 'mk_macaron_d1_jaxref_r8_df95d6'

def setup_inputs(seed: int=0):
    np.random.seed(seed)
    _w = jnp.asarray

    def _L0_attn_setup():
        import jax, jax.numpy as jnp
        import numpy as np
        HID = 256
        NH = 32
        DK = 128
        DV = 256
        HQK = DK // NH
        HV = DV // NH
        RLO = 32
        GLO = 64
        EPS = 1e-05
        B, L = (4, 512)

        def _forward(x, mu_x, Wx1, Wx2, Wr, Ww1, Ww2, bw, Wk, Wv, Wg, bonus, gn_w, gn_b, Wo):
            Bn, Ln, _ = x.shape
            delta = jnp.pad(x[:, :-1], ((0, 0), (1, 0), (0, 0))) - x
            z = jnp.tanh((x + delta * mu_x) @ Wx1).reshape(Bn, Ln, 5, RLO)
            mus = jnp.einsum('blnr,nrd->blnd', z, Wx2)
            mr, mw, mk, mv, mg = (mus[:, :, i] for i in range(5))
            r = (x + delta * mr) @ Wr
            w = jnp.tanh((x + delta * mw) @ Ww1) @ Ww2 + bw
            k = (x + delta * mk) @ Wk
            v = (x + delta * mv) @ Wv
            g = (x + delta * mg) @ Wg
            heads = lambda t, d: t.reshape(Bn, Ln, NH, d).transpose(1, 0, 2, 3)
            r_t, k_t = (heads(r, HQK), heads(k, HQK))
            v_t = heads(v, HV)
            decay = jnp.exp(-jnp.exp(heads(w, HQK)))

            def step(S, inp):
                rt, kt, vt, dt = inp
                kv = kt[..., :, None] * vt[..., None, :]
                ot = jnp.einsum('bhk,bhkv->bhv', rt, S + bonus[None, :, :, None] * kv)
                return (S * dt[..., :, None] + kv, ot)
            S0 = jnp.zeros((Bn, NH, HQK, HV), x.dtype)
            _, o = jax.lax.scan(step, S0, (r_t, k_t, v_t, decay))
            o = o.transpose(1, 0, 2, 3)
            mean = o.mean(-1, keepdims=True)
            var = o.var(-1, keepdims=True)
            on = (o - mean) * jax.lax.rsqrt(var + EPS) * gn_w + gn_b
            gh = g.reshape(Bn, Ln, NH, HV)
            o = on * (gh * jax.nn.sigmoid(gh))
            return o.reshape(Bn, Ln, DV) @ Wo
        key = jax.random.key(seed)
        ks = jax.random.split(key, 16)
        s = 0.02
        return {'hidden_states': jax.random.normal(ks[0], (B, L, HID), jnp.float32), 'mu_x': jax.random.uniform(ks[1], (HID,), jnp.float32), 'Wx1': jax.random.normal(ks[2], (HID, 5 * RLO), jnp.float32) * s, 'Wx2': jax.random.normal(ks[3], (5, RLO, HID), jnp.float32) * s, 'Wr': jax.random.normal(ks[4], (HID, DK), jnp.float32) * s, 'Ww1': jax.random.normal(ks[5], (HID, GLO), jnp.float32) * s, 'Ww2': jax.random.normal(ks[6], (GLO, DK), jnp.float32) * s, 'bw': jnp.zeros((DK,), jnp.float32), 'Wk': jax.random.normal(ks[7], (HID, DK), jnp.float32) * s, 'Wv': jax.random.normal(ks[8], (HID, DV), jnp.float32) * s, 'Wg': jax.random.normal(ks[9], (HID, DV), jnp.float32) * s, 'bonus': jax.random.normal(ks[10], (NH, HQK), jnp.float32) * s, 'gn_w': jnp.ones((HV,), jnp.float32), 'gn_b': jnp.zeros((HV,), jnp.float32), 'Wo': jax.random.normal(ks[11], (DV, HID), jnp.float32) * s}
    _L0_attn_in = _L0_attn_setup()

    def _L0_ffn_setup():
        import jax, jax.numpy as jnp
        import numpy as np
        DIM = 256
        HID = 704
        ZERO_POINT = 128.0

        def _qlinear(x, wq, scale):
            W = (wq.astype(jnp.float32) - ZERO_POINT) * scale[:, None]
            return jnp.einsum('bsd,hd->bsh', x, W)
        key = jax.random.key(seed)
        ks = jax.random.split(key, 7)
        B, S = (4, 256)
        sg = jax.random.uniform(ks[1], (HID,)) * (0.02 / np.sqrt(DIM)) + 0.0001
        su = jax.random.uniform(ks[3], (HID,)) * (0.02 / np.sqrt(DIM)) + 0.0001
        sd = jax.random.uniform(ks[5], (DIM,)) * (0.02 / np.sqrt(HID)) + 0.0001
        return {'x': jax.random.normal(ks[0], (B, S, DIM), dtype=jnp.float32), 'wq_gate': jax.random.randint(ks[2], (HID, DIM), 0, 32, dtype=jnp.int32), 's_gate': sg, 'wq_up': jax.random.randint(ks[4], (HID, DIM), 0, 32, dtype=jnp.int32), 's_up': su, 'wq_down': jax.random.randint(ks[6], (DIM, HID), 0, 32, dtype=jnp.int32), 's_down': sd}
    _L0_ffn_in = _L0_ffn_setup()
    _d = {'L0_attn_hidden_states': _L0_attn_in['hidden_states'], 'L0_attn_mu_x': _L0_attn_in['mu_x'], 'L0_attn_Wx1': _L0_attn_in['Wx1'], 'L0_attn_Wx2': _L0_attn_in['Wx2'], 'L0_attn_Wr': _L0_attn_in['Wr'], 'L0_attn_Ww1': _L0_attn_in['Ww1'], 'L0_attn_Ww2': _L0_attn_in['Ww2'], 'L0_attn_bw': _L0_attn_in['bw'], 'L0_attn_Wk': _L0_attn_in['Wk'], 'L0_attn_Wv': _L0_attn_in['Wv'], 'L0_attn_Wg': _L0_attn_in['Wg'], 'L0_attn_bonus': _L0_attn_in['bonus'], 'L0_attn_gn_w': _L0_attn_in['gn_w'], 'L0_attn_gn_b': _L0_attn_in['gn_b'], 'L0_attn_Wo': _L0_attn_in['Wo'], 'L0_ffn_wq_gate': _L0_ffn_in['wq_gate'], 'L0_ffn_s_gate': _L0_ffn_in['s_gate'], 'L0_ffn_wq_up': _L0_ffn_in['wq_up'], 'L0_ffn_s_up': _L0_ffn_in['s_up'], 'L0_ffn_wq_down': _L0_ffn_in['wq_down'], 'L0_ffn_s_down': _L0_ffn_in['s_down']}
    _x0 = _d['L0_attn_hidden_states']
    _d['L0_attn_hidden_states'] = jax.random.normal(jax.random.fold_in(jax.random.key(seed), 1), (1, 1024, 256), dtype=_x0.dtype)
    del _x0
    return _d

def reference(L0_attn_hidden_states, L0_attn_mu_x, L0_attn_Wx1, L0_attn_Wx2, L0_attn_Wr, L0_attn_Ww1, L0_attn_Ww2, L0_attn_bw, L0_attn_Wk, L0_attn_Wv, L0_attn_Wg, L0_attn_bonus, L0_attn_gn_w, L0_attn_gn_b, L0_attn_Wo, L0_ffn_wq_gate, L0_ffn_s_gate, L0_ffn_wq_up, L0_ffn_s_up, L0_ffn_wq_down, L0_ffn_s_down):

    def _L0_attn_ref(hidden_states, mu_x, Wx1, Wx2, Wr, Ww1, Ww2, bw, Wk, Wv, Wg, bonus, gn_w, gn_b, Wo):
        import jax, jax.numpy as jnp
        import numpy as np
        HID = 256
        NH = 32
        DK = 128
        DV = 256
        HQK = DK // NH
        HV = DV // NH
        RLO = 32
        GLO = 64
        EPS = 1e-05
        B, L = (4, 512)

        def _forward(x, mu_x, Wx1, Wx2, Wr, Ww1, Ww2, bw, Wk, Wv, Wg, bonus, gn_w, gn_b, Wo):
            Bn, Ln, _ = x.shape
            delta = jnp.pad(x[:, :-1], ((0, 0), (1, 0), (0, 0))) - x
            z = jnp.tanh((x + delta * mu_x) @ Wx1).reshape(Bn, Ln, 5, RLO)
            mus = jnp.einsum('blnr,nrd->blnd', z, Wx2)
            mr, mw, mk, mv, mg = (mus[:, :, i] for i in range(5))
            r = (x + delta * mr) @ Wr
            w = jnp.tanh((x + delta * mw) @ Ww1) @ Ww2 + bw
            k = (x + delta * mk) @ Wk
            v = (x + delta * mv) @ Wv
            g = (x + delta * mg) @ Wg
            heads = lambda t, d: t.reshape(Bn, Ln, NH, d).transpose(1, 0, 2, 3)
            r_t, k_t = (heads(r, HQK), heads(k, HQK))
            v_t = heads(v, HV)
            decay = jnp.exp(-jnp.exp(heads(w, HQK)))

            def step(S, inp):
                rt, kt, vt, dt = inp
                kv = kt[..., :, None] * vt[..., None, :]
                ot = jnp.einsum('bhk,bhkv->bhv', rt, S + bonus[None, :, :, None] * kv)
                return (S * dt[..., :, None] + kv, ot)
            S0 = jnp.zeros((Bn, NH, HQK, HV), x.dtype)
            _, o = jax.lax.scan(step, S0, (r_t, k_t, v_t, decay))
            o = o.transpose(1, 0, 2, 3)
            mean = o.mean(-1, keepdims=True)
            var = o.var(-1, keepdims=True)
            on = (o - mean) * jax.lax.rsqrt(var + EPS) * gn_w + gn_b
            gh = g.reshape(Bn, Ln, NH, HV)
            o = on * (gh * jax.nn.sigmoid(gh))
            return o.reshape(Bn, Ln, DV) @ Wo
        return _forward(hidden_states, mu_x, Wx1, Wx2, Wr, Ww1, Ww2, bw, Wk, Wv, Wg, bonus, gn_w, gn_b, Wo)

    def _L0_ffn_ref(x, wq_gate, s_gate, wq_up, s_up, wq_down, s_down):
        import jax, jax.numpy as jnp
        import numpy as np
        DIM = 256
        HID = 704
        ZERO_POINT = 128.0

        def _qlinear(x, wq, scale):
            W = (wq.astype(jnp.float32) - ZERO_POINT) * scale[:, None]
            return jnp.einsum('bsd,hd->bsh', x, W)
        gate = _qlinear(x, wq_gate, s_gate)
        gate = jax.nn.silu(gate)
        up = _qlinear(x, wq_up, s_up)
        return _qlinear(gate * up, wq_down, s_down)
    x = L0_attn_hidden_states
    x = x + 0.5 * _L0_ffn_ref(_layernorm(x, axis=-1), L0_ffn_wq_gate, L0_ffn_s_gate, L0_ffn_wq_up, L0_ffn_s_up, L0_ffn_wq_down, L0_ffn_s_down)
    x = x + _L0_attn_ref(_layernorm(x, axis=-1), L0_attn_mu_x, L0_attn_Wx1, L0_attn_Wx2, L0_attn_Wr, L0_attn_Ww1, L0_attn_Ww2, L0_attn_bw, L0_attn_Wk, L0_attn_Wv, L0_attn_Wg, L0_attn_bonus, L0_attn_gn_w, L0_attn_gn_b, L0_attn_Wo)
    x = x + 0.5 * _L0_ffn_ref(_layernorm(x, axis=-1), L0_ffn_wq_gate, L0_ffn_s_gate, L0_ffn_wq_up, L0_ffn_s_up, L0_ffn_wq_down, L0_ffn_s_down)
    return x

_drawn_inputs = setup_inputs


def setup_inputs(seed=0):
    import zlib

    import numpy as np

    out = dict(_drawn_inputs(seed))
    spreads = {'L0_attn_bw': (0.0, 2.0), 'L0_attn_gn_w': (1.0, 0.6), 'L0_attn_gn_b': (0.0, 0.8)}
    factors = {'L0_attn_mu_x': 8.0,
     'L0_attn_Wx1': 8.0,
     'L0_attn_Wx2': 8.0,
     'L0_attn_Ww1': 25.301,
     'L0_attn_Ww2': 25.427,
     'L0_attn_bonus': 28.291,
     'L0_ffn_s_gate': 8.0,
     'L0_ffn_s_up': 8.0,
     'L0_ffn_s_down': 8.0}
    for name, (base, spread) in spreads.items():
        noise = np.random.default_rng([zlib.crc32(name.encode()), seed]).standard_normal(out[name].shape)
        drawn = base * np.exp(spread * noise) if base else spread * noise
        out[name] = jnp.asarray(drawn.astype(out[name].dtype))
    for name, factor in factors.items():
        out[name] = (out[name] * factor).astype(out[name].dtype)
    return out
```

```python
from contextlib import ExitStack

import concourse.bass as bass
import numpy as np
from concourse import mybir

T, D, F = 1024, 256, 704
P = 128
HALVES = 2
TH = T // HALVES
SUB = TH // P
KC = D // P
FULL = F // P
REM = F - FULL * P
FC = FULL + 1
NH, HQK, HV = 32, 4, 8
PLANES = HV
RLO, GLO, MIX = 32, 64, 5
EPS = 1e-5
ZERO_POINT = 128.0

C_SG, C_SU, C_MU, C_BW, C_BONUS, C_GNW, C_GNB = 0, FC, 2 * FC, 2 * FC + 2, 2 * FC + 3, 2 * FC + 4, 2 * FC + 6
C_ALL = 2 * FC + 8

MIXES = ["w", "v", "k", "r", "g"]
INDEX = {"r": 0, "w": 1, "k": 2, "v": 3, "g": 4}
PLANE_ORDER = [p for q in range(4) for p in (q, q + 4)]
POOL_PLANES = (4, 5, 6, 7)


def macaron(nc, x, wgu, wd, table, sdown, wx1, wx2, wr, wk, wv, wg, ww1, ww2, wo, ident, rep, out):
    fp32, fp32r, int32 = mybir.dt.float32, mybir.dt.float32r, mybir.dt.int32
    ALU, ACT, AX = mybir.AluOpType, mybir.ActivationFunctionType, mybir.AxisListType
    ctx = ExitStack()
    with ctx:
        def sb(name, shape, dt=fp32):
            return ctx.enter_context(nc.sbuf_tensor(name, shape, dt))

        def sem(name):
            return ctx.enter_context(nc.semaphore(name))

        xs = sb("xs", [P, T // P, D])
        tab = sb("tab", [P, C_ALL])
        sdn = sb("sdn", [P, D])
        idt = sb("idt", [P, P])
        rept = sb("rept", [P, P])
        minus_half = sb("minus_half", [P, SUB])
        wgu_int = sb("wgu_int", [P, KC, (2 * FULL + 1) * P], int32)
        wgu_r = sb("wgu_r", [P, KC, (2 * FULL + 1) * P], fp32r)
        wd_int = sb("wd_int", [P, FC, D], int32)
        wd_r = sb("wd_r", [P, FC, D], fp32r)
        wx1s = sb("wx1s", [P, KC, MIX * RLO])
        wx2s = sb("wx2s", [P, D])
        wx2last = sb("wx2last", [P, D])
        wrs = sb("wrs", [P, KC, P])
        wks = sb("wks", [P, KC, P])
        wvs = sb("wvs", [P, KC, D])
        wgs = sb("wgs", [P, KC, D])
        ww1s = sb("ww1s", [P, KC, GLO])
        ww2s = sb("ww2s", [GLO, P])
        wos = sb("wos", [P, KC, D])

        stats = sb("stats", [P, 6, SUB, 6])
        mv = sb("mv", [P, 6, SUB, 2])
        var_eps = sb("var_eps", [P, 6, SUB])
        rstd = sb("rstd", [P, 6, SUB])
        xn = sb("xn", [P, 2, SUB, D])

        xhi = sb("xhi", [P, 2, KC, TH], fp32r)
        xlo = sb("xlo", [P, 2, KC, TH], fp32r)
        silu = sb("silu", [P, 2, TH])
        hf = sb("hf", [P, 2, TH])
        hhi = sb("hhi", [P, FC, TH], fp32r)
        hlo = sb("hlo", [P, FC, TH], fp32r)
        ffn_out = sb("ffn_out", [P, 2 * D])

        xlt = sb("xlt", [P, KC, T + 1])
        delta = sb("delta", [P, KC, TH])
        xmu = sb("xmu", [P, KC, TH])
        zt = sb("zt", [P, TH])
        mix = sb("mix", [P, 3, KC, TH])
        decay = sb("decay", [P, 2, TH])
        kt = sb("kt", [P, 2, TH])
        rt = sb("rt", [P, 2, TH])
        sg = sb("sg", [P, 2, KC, TH])
        bonus_v = sb("bonus_v", [P, KC, TH])
        vrep = sb("vrep", [P, PLANES, TH])
        state = sb("state", [P, PLANES, TH + 1])
        vsum = sb("vsum", [P, SUB, NH])
        oc = sb("oc", [P, SUB, D])
        ssum = sb("ssum", [P, SUB, NH])
        gstd = sb("gstd", [P, SUB, NH])

        old_wgu = wgu_int[:, :, :].bitcast(fp32).rearrange("p c f -> p (c f)")
        old_wd = wd_int[:, :, :].bitcast(fp32).rearrange("p c d -> p (c d)")
        vt = old_wgu[:, 0:KC * TH].rearrange("p (c t) -> p c t", t=TH)
        ot = old_wgu[:, KC * TH:2 * KC * TH].rearrange("p (c t) -> p c t", t=TH)
        gated = ot
        tw = old_wgu[0:GLO, 2 * KC * TH:(2 * KC + 1) * TH]
        ztlast = old_wgu[P - RLO:P, 2 * KC * TH:(2 * KC + 1) * TH]
        osq = old_wd[:, 0:SUB * D].rearrange("p (s d) -> p s d", d=D)
        ogn = old_wd[:, 0:KC * TH].rearrange("p (c t) -> p c t", t=TH)
        rbk = old_wd[:, KC * TH:(KC + 1) * TH]

        bank = [ctx.enter_context(nc.psum_tensor(f"bank{b}", [P, TH], fp32)) for b in range(8)]
        bank_full = [sem(f"bank_full{b}") for b in range(8)]
        bank_free = [sem(f"bank_free{b}") for b in range(8)]

        x_in = [sem(f"x_in{h}") for h in range(HALVES)]
        wgu_in = [sem(f"wgu_in{q}") for q in range(3)]
        wd_in = sem("wd_in")
        tab_in = sem("tab_in")
        sdn_in = sem("sdn_in")
        idt_in = sem("idt_in")
        wz_in = sem("wz_in")
        wp_in = sem("wp_in")
        stored = sem("stored")
        vrep_in = [[sem(f"vrep_in{h}_{q}") for q in range(4)] for h in range(HALVES)]
        wgu_ready = sem("wgu_ready")
        wd_ready = sem("wd_ready")
        wd_last_ready = sem("wd_last_ready")
        consts = sem("consts")
        dve_seq = sem("dve_seq")
        act_seq = sem("act_seq")
        var_ready = sem("var_ready")
        rstd_ready = sem("rstd_ready")
        xn_ready = sem("xn_ready")
        xhi_ready = sem("xhi_ready")
        xlo_ready = sem("xlo_ready")
        silu_ready = sem("silu_ready")
        hf_ready = sem("hf_ready")
        hhi_ready = sem("hhi_ready")
        hlo_ready = sem("hlo_ready")
        hlo_last_ready = sem("hlo_last_ready")
        down_done = sem("down_done")
        ffn_out_ready = sem("ffn_out_ready")
        residual_ready = sem("residual_ready")
        attn_added = sem("attn_added")
        xlt_ready = sem("xlt_ready")
        xmu_ready = sem("xmu_ready")
        z_ready = sem("z_ready")
        scaled_ready = sem("scaled_ready")
        mix_ready = sem("mix_ready")
        tw_ready = sem("tw_ready")
        decay_ready = sem("decay_ready")
        v_ready = sem("v_ready")
        k_ready = sem("k_ready")
        r_ready = sem("r_ready")
        sg_ready = sem("sg_ready")
        rbk_ready = sem("rbk_ready")
        bonus_v_ready = sem("bonus_v_ready")
        scan_ready = sem("scan_ready")
        read_ready = [sem("read_ready_dve"), sem("read_ready_pool")]
        ot_ready = sem("ot_ready")
        oc_ready = sem("oc_ready")
        osq_ready = sem("osq_ready")
        gvar_ready = sem("gvar_ready")
        gstd_ready = sem("gstd_ready")
        on_ready = sem("on_ready")
        ogn_ready = sem("ogn_ready")
        gated_ready = sem("gated_ready")

        fills = {}
        filled = [0] * 8

        def full(eng, name):
            b, n = fills[name]
            eng.wait_ge(bank_full[b], n + 1)
            return bank[b]

        def free(name):
            return bank_free[fills[name][0]]

        block = ctx.enter_context(nc.Block())

        @block.tensor
        def _(pe):
            def take(b, name):
                n = filled[b]
                if n:
                    pe.wait_ge(bank_free[b], n)
                fills[name] = (b, n)
                filled[b] += 1
                return bank[b]

            turn = [0]

            def take_next(name):
                b = turn[0] % 4
                turn[0] += 1
                return take(b, name)

            def done(ins, name):
                ins.then_inc(bank_full[fills[name][0]], 1)

            def transpose_x(l):
                pe.wait_ge(xn_ready, l + 1)
                for c in range(KC):
                    b = take(6 + c, ("xT", l, c))
                    for s in range(SUB):
                        ins = pe.transpose(b[:, s * P:(s + 1) * P], xn[:, l % 2, s, c * P:(c + 1) * P], idt[:, :])
                    done(ins, ("xT", l, c))

            def gate_up(u, j):
                if u == 0:
                    pe.wait_ge(wgu_ready, j // 2 + 1)
                for what in (("gate", "up") if j < FULL else ("both",)):
                    w = (2 * j + (what == "up")) * P
                    b = take_next((what, u, j))
                    for n, part in enumerate((xhi, xlo)):
                        if j == 0 and what == "gate":
                            pe.wait_ge((xhi_ready, xlo_ready)[n], KC * (u + 1))
                        for c in range(KC):
                            ins = pe.matmul(b[:, :], wgu_r[:, c, w:w + P], part[:, u % 2, c, :],
                                            start=(n == 0 and c == 0), stop=(n == 1 and c == KC - 1))
                    done(ins, (what, u, j))

            def down(u, j):
                if j == 0:
                    if u == 0:
                        pe.wait_ge(wd_ready, 1)
                    take(4, ("down", u, 0))
                    take(5, ("down", u, 1))
                lo = 0 if j < FULL else P - REM
                if u == 0 and j == FULL:
                    pe.wait_ge(wd_last_ready, 1)
                for n, part in enumerate((hhi, hlo)):
                    if n == 0:
                        pe.wait_ge(hhi_ready, FC * u + j + 1)
                    elif j < FULL:
                        pe.wait_ge(hlo_ready, FULL * u + j + 1)
                    else:
                        pe.wait_ge(hlo_last_ready, u + 1)
                    for s in range(SUB):
                        first = j == 0 and n == 0 and s % 2 == 0
                        ins = pe.matmul(bank[4 + s // 2][:, (s % 2) * D:(s % 2 + 1) * D],
                                        part[lo:P, j, s * P:(s + 1) * P], wd_r[lo:P, j, :],
                                        start=first, stop=(j == FC - 1 and n == 1),
                                        skip_group_check=True)
                ins.then_inc(down_done, 1)

            def low_rank(h):
                pe.wait_ge(xmu_ready, KC * (h + 1))
                for name, lo, hi in (("z", 0, P), ("zlast", P, MIX * RLO)):
                    b = take_next((name, h))
                    for c in range(KC):
                        ins = pe.matmul(b[0:hi - lo, :], wx1s[:, c, lo:hi], xmu[:, c, :],
                                        start=(c == 0), stop=(c == KC - 1))
                    done(ins, (name, h))

            def mix_rate(h, m):
                i = INDEX[m]
                pe.wait_ge(z_ready, 2 * h + (1 if i < 4 else 2))
                for c in range(KC):
                    b = take_next(("rate", h, m, c))
                    if i < 4:
                        w, z = wx2s[i * RLO:(i + 1) * RLO, c * P:(c + 1) * P], zt[i * RLO:(i + 1) * RLO, :]
                    else:
                        w, z = wx2last[P - RLO:P, c * P:(c + 1) * P], ztlast
                    done(pe.matmul(b[:, :], w, z, start=True, stop=True), ("rate", h, m, c))

            def project(h, m):
                w, outs = {"w": (ww1s, (GLO,)), "v": (wvs, (P, P)), "k": (wks, (P,)),
                           "r": (wrs, (P,)), "g": (wgs, (P, P))}[m]
                n = 5 * h + MIXES.index(m)
                pe.wait_ge(mix_ready, KC * (n + 1))
                for o, rows in enumerate(outs):
                    b = take_next((m, h, o))
                    for c in range(KC):
                        ins = pe.matmul(b[0:rows, :], w[:, c, o * P:o * P + rows], mix[:, n % 3, c, :],
                                        start=(c == 0), stop=(c == KC - 1))
                    done(ins, (m, h, o))

            def decay_logit(h):
                pe.wait_ge(tw_ready, h + 1)
                b = take_next(("w2", h))
                done(pe.matmul(b[:, :], ww2s[:, :], tw, start=True, stop=True), ("w2", h))

            def bonus_sum(h):
                pe.wait_ge(rbk_ready, h + 1)
                b = take_next(("bonus", h))
                done(pe.matmul(b[:, :], rept[:, :], rbk, start=True, stop=True), ("bonus", h))

            counts = [0, 0]

            def key_sum(h, p):
                c, q = p // 4, p % 4
                if q == 0:
                    take(6 + c, ("o", h, c))
                who = int(p in POOL_PLANES)
                counts[who] += 1
                pe.wait_ge(read_ready[who], counts[who])
                ins = pe.matmul(bank[6 + c][q * NH:(q + 1) * NH, :], rept[:, 0:NH], vrep[:, p, :],
                                start=True, stop=True)
                if q == 3:
                    done(ins, ("o", h, c))

            def o_token_major(h):
                pe.wait_ge(ot_ready, KC * (h + 1))
                for g in range(2):
                    b = take(6 + g, ("otm", h, g))
                    for s in range(2):
                        for c in range(KC):
                            at = (2 * g + s) * P
                            ins = pe.transpose(b[:, s * D + c * P:s * D + (c + 1) * P], ot[:, c, at:at + P], idt[:, :])
                    done(ins, ("otm", h, g))

            def o_feature_major(h):
                pe.wait_ge(on_ready, h + 1)
                for c in range(KC):
                    b = take(6 + c, ("ofm", h, c))
                    for s in range(SUB):
                        ins = pe.transpose(b[:, s * P:(s + 1) * P], oc[:, s, c * P:(c + 1) * P], idt[:, :])
                    done(ins, ("ofm", h, c))

            def output(h):
                pe.wait_ge(gated_ready, KC * (h + 1))
                for g in range(2):
                    b = take(6 + g, ("attn", h, g))
                    for s in range(2):
                        for c in range(KC):
                            at = (2 * g + s) * P
                            ins = pe.matmul(b[:, s * D:(s + 1) * D], gated[:, c, at:at + P], wos[:, c, :],
                                            start=(c == 0), stop=(c == KC - 1))
                    done(ins, ("attn", h, g))

            pe.wait_ge(idt_in, 32)
            transpose_x(0)
            gate_up(0, 0); gate_up(0, 1); gate_up(0, 2); down(0, 0); gate_up(0, 3); down(0, 1)
            gate_up(0, 4); down(0, 2); gate_up(0, 5); transpose_x(1); down(0, 3); gate_up(1, 0)
            down(0, 4); gate_up(1, 1); down(0, 5)
            gate_up(1, 2); down(1, 0); gate_up(1, 3); down(1, 1); transpose_x(2)
            gate_up(1, 4); down(1, 2); gate_up(1, 5); down(1, 3)
            pe.wait_ge(wz_in, 48)
            low_rank(0); down(1, 4); mix_rate(0, "w"); down(1, 5)
            mix_rate(0, "v"); mix_rate(0, "k")
            pe.wait_ge(wp_in, 112)
            project(0, "w"); project(0, "v"); transpose_x(3); mix_rate(0, "r"); project(0, "k")
            decay_logit(0); mix_rate(0, "g"); project(0, "r"); low_rank(1); project(0, "g")
            mix_rate(1, "w"); bonus_sum(0); mix_rate(1, "v"); key_sum(0, 0); key_sum(0, 4)
            mix_rate(1, "k"); project(1, "w"); key_sum(0, 1); key_sum(0, 5); project(1, "v")
            mix_rate(1, "r"); project(1, "k"); key_sum(0, 2); key_sum(0, 6); decay_logit(1)
            mix_rate(1, "g"); project(1, "r"); key_sum(0, 3); key_sum(0, 7)
            project(1, "g"); o_token_major(0); bonus_sum(1); o_feature_major(0); output(0)
            transpose_x(4)
            gate_up(2, 0); key_sum(1, 0); key_sum(1, 4); gate_up(2, 1); key_sum(1, 1); key_sum(1, 5)
            gate_up(2, 2); down(2, 0); key_sum(1, 2); key_sum(1, 6); gate_up(2, 3); down(2, 1)
            key_sum(1, 3); key_sum(1, 7); gate_up(2, 4); down(2, 2); o_token_major(1)
            gate_up(2, 5); down(2, 3); down(2, 4); o_feature_major(1); down(2, 5); output(1)
            transpose_x(5)
            gate_up(3, 0); gate_up(3, 1); gate_up(3, 2); down(3, 0); gate_up(3, 3); down(3, 1)
            gate_up(3, 4); down(3, 2); gate_up(3, 5); down(3, 3); down(3, 4); down(3, 5)

        @block.vector
        def _(dve):
            steps = [0]

            def step(ins):
                steps[0] += 1
                ins.then_inc(dve_seq, 1)

            def settle():
                dve.wait_ge(dve_seq, steps[0])

            def col(c, rows=slice(0, P)):
                return tab[rows, c:c + 1]

            def norm_stats(l):
                h = l % 2
                if l < 2:
                    dve.wait_ge(x_in[h], 16)
                elif l < 4:
                    dve.wait_ge(residual_ready, 2 * (h + 1))
                else:
                    dve.wait_ge(attn_added, 2 * (h + 1))
                for s in range(SUB):
                    step(dve.bn_stats(stats[:, l, s, :], xs[:, SUB * h + s, :]))
                settle()
                for s in range(SUB):
                    step(dve.bn_aggr(mv[:, l, s, :], stats[:, l, s, :]))
                settle()
                dve.tensor_scalar(var_eps[:, l, :], mv[:, l, :, 1], EPS, None, ALU.add).then_inc(var_ready, 1)

            def normalise(l):
                h = l % 2
                dve.wait_ge(rstd_ready, l + 1)
                if l >= 2:
                    full(dve, ("xT", l - 2, 1))
                for s in range(SUB):
                    ins = dve.tensor_scalar(xn[:, l % 2, s, :], xs[:, SUB * h + s, :], mv[:, l, s, 0:1],
                                            rstd[:, l, s:s + 1], ALU.subtract, ALU.mult)
                ins.then_inc(xn_ready, 1)

            def split_x(u):
                l = u if u < 2 else u + 2
                for c in range(KC):
                    dve.wait_ge(xhi_ready, KC * u + c + 1)
                    b = full(dve, ("xT", l, c))
                    dve.tensor_tensor(xlo[:, u % 2, c, :], b[:, :], xhi[:, u % 2, c, :].bitcast(fp32),
                                      ALU.subtract).then_inc(xlo_ready, 1)
                    dve.wait_ge(xlo_ready, KC * u + c + 1)
                    dve.sem_inc(bank_free[6 + c], 1)

            def hidden(u, j):
                n = FC * u + j
                dve.wait_ge(silu_ready, n + 1)
                if n >= 2 and (n - 2) % FC < FULL:
                    dve.wait_ge(hlo_ready, FULL * ((n - 2) // FC) + (n - 2) % FC + 1)
                name = ("up" if j < FULL else "both", u, j)
                b = full(dve, name)
                rows = slice(0, P) if j < FULL else slice(P - REM, P)
                dve.scalar_tensor_tensor(hf[rows, n % 2, :], b[rows, :], col(C_SU + j, rows), silu[rows, n % 2, :],
                                         ALU.mult, ALU.mult).then_inc(hf_ready, 1)
                dve.wait_ge(hf_ready, n + 1)
                dve.sem_inc(free(name), 1)

            def low_last(u):
                n = FC * u + FULL
                dve.wait_ge(hhi_ready, n + 1)
                if u:
                    dve.wait_ge(down_done, FC * u)
                rows = slice(P - REM, P)
                dve.tensor_tensor(hlo[rows, FULL, :], hf[rows, n % 2, :], hhi[rows, FULL, :].bitcast(fp32),
                                  ALU.subtract).then_inc(hlo_last_ready, 1)

            def scale_down(u):
                dve.wait_ge(down_done, FC * (u + 1))
                if u == 0:
                    dve.wait_ge(consts, 3)
                for g in range(2):
                    if u or g:
                        dve.wait_ge(residual_ready, 2 * u + g)
                    dve.tensor_tensor(ffn_out[:, :].rearrange("p (s d) -> p s d", d=D),
                                      bank[4 + g][:, :].rearrange("p (s d) -> p s d", d=D),
                                      sdn[:, :].unsqueeze(1).to_broadcast([P, 2, D]),
                                      ALU.mult).then_inc(ffn_out_ready, 1)
                    dve.wait_ge(ffn_out_ready, 2 * u + g + 1)
                    dve.sem_inc(bank_free[4 + g], 1)

            def shift(h):
                dve.wait_ge(xlt_ready, KC * (h + 1))
                at = TH * h
                step(dve.tensor_tensor(delta[:, :, :], xlt[:, :, at:at + TH], xlt[:, :, at + 1:at + TH + 1],
                                       ALU.subtract))
                settle()
                if h:
                    full(dve, ("zlast", h - 1))
                for c in range(KC):
                    dve.scalar_tensor_tensor(xmu[:, c, :], delta[:, c, :], col(C_MU + c),
                                             xlt[:, c, at + 1:at + TH + 1], ALU.mult, ALU.add).then_inc(xmu_ready, 1)

            def scale_delta(h, m):
                n = 5 * h + MIXES.index(m)
                if n >= 3:
                    was = MIXES[(n - 3) % 5]
                    full(dve, (was, (n - 3) // 5, 1 if was in "vg" else 0))
                for c in range(KC):
                    b = full(dve, ("rate", h, m, c))
                    dve.tensor_tensor(mix[:, n % 3, c, :], b[:, :], delta[:, c, :], ALU.mult).then_inc(scaled_ready, 1)
                    dve.wait_ge(scaled_ready, KC * n + c + 1)
                    dve.sem_inc(free(("rate", h, m, c)), 1)

            def bonus_in(h):
                dve.wait_ge(r_ready, h + 1)
                dve.wait_ge(k_ready, h + 1)
                dve.scalar_tensor_tensor(rbk, rt[:, h, :], col(C_BONUS), kt[:, h, :],
                                         ALU.mult, ALU.mult).then_inc(rbk_ready, 1)

            def bonus_out(h):
                b = full(dve, ("bonus", h))
                for c in range(KC):
                    dve.tensor_tensor(bonus_v[:, c, :], b[:, :], vt[:, c, :], ALU.mult).then_inc(bonus_v_ready, 1)
                dve.wait_ge(bonus_v_ready, KC * (h + 1))
                dve.sem_inc(free(("bonus", h)), 1)

            reads = [0]

            def plane(h, p):
                dve.wait_ge(vrep_in[h][p % 4], 64)
                dve.wait_ge(decay_ready, h + 1)
                dve.wait_ge(k_ready, h + 1)
                step(dve.tensor_tensor(vrep[:, p, :], kt[:, h, :], vrep[:, p, :], ALU.mult))
                settle()
                dve.tensor_tensor_scan(state[:, p, 1:TH + 1], decay[:, h, :], vrep[:, p, :],
                                       state[:, p, 0:1], ALU.mult, ALU.add).then_inc(scan_ready, 1)
                if p not in POOL_PLANES:
                    reads[0] += 1
                    dve.wait_ge(scan_ready, PLANES * h + PLANE_ORDER.index(p) + 1)
                    dve.wait_ge(r_ready, h + 1)
                    dve.tensor_tensor(vrep[:, p, :], rt[:, h, :], state[:, p, 0:TH],
                                      ALU.mult).then_inc(read_ready[0], 1)

            def carry_states():
                dve.wait_ge(read_ready[1], len(POOL_PLANES))
                step(dve.tensor_copy(state[:, :, 0:1], state[:, :, TH:TH + 1]))

            def add_bonus(h):
                for c in range(KC):
                    b = full(dve, ("o", h, c))
                    dve.tensor_tensor(ot[:, c, :], b[:, :], bonus_v[:, c, :], ALU.add).then_inc(ot_ready, 1)
                    dve.wait_ge(ot_ready, KC * h + c + 1)
                    dve.sem_inc(bank_free[6 + c], 1)

            def centre(h):
                for g in range(2):
                    b = full(dve, ("otm", h, g))
                    step(dve.tensor_reduce(vsum[:, 2 * g:2 * g + 2, :],
                                           b[:, :].rearrange("p (s v n) -> p s n v", s=2, n=NH), AX.X, ALU.add))
                settle()
                step(dve.tensor_scalar(vsum[:, :, :], vsum[:, :, :], 1.0 / HV, None, ALU.mult))
                settle()
                for g in range(2):
                    b = full(dve, ("otm", h, g))
                    dve.tensor_tensor(oc[:, 2 * g:2 * g + 2, :].rearrange("p s (v n) -> p s v n", n=NH),
                                      b[:, :].rearrange("p (s v n) -> p s v n", s=2, n=NH),
                                      vsum[:, 2 * g:2 * g + 2, :].unsqueeze(2).to_broadcast([P, 2, HV, NH]),
                                      ALU.subtract).then_inc(oc_ready, 1)
                    dve.wait_ge(oc_ready, 2 * h + g + 1)
                    dve.sem_inc(bank_free[6 + g], 1)

            def head_var(h):
                dve.wait_ge(osq_ready, h + 1)
                step(dve.tensor_reduce(ssum[:, :, :], osq[:, :, :].rearrange("p s (v n) -> p s n v", n=NH),
                                       AX.X, ALU.add))
                settle()
                dve.tensor_scalar(ssum[:, :, :], ssum[:, :, :], 1.0 / HV, EPS, ALU.mult, ALU.add).then_inc(gvar_ready, 1)

            def head_scale(h):
                dve.wait_ge(gstd_ready, h + 1)
                step(dve.reciprocal(gstd[:, :, :], gstd[:, :, :]))
                settle()
                dve.tensor_tensor(oc[:, :, :].rearrange("p s (v n) -> p s v n", n=NH),
                                  oc[:, :, :].rearrange("p s (v n) -> p s v n", n=NH),
                                  gstd[:, :, :].unsqueeze(2).to_broadcast([P, SUB, HV, NH]),
                                  ALU.mult).then_inc(on_ready, 1)

            def gate_o(h):
                for c in range(KC):
                    dve.wait_ge(ogn_ready, KC * h + c + 1)
                    dve.wait_ge(sg_ready, KC * (h + 1))
                    dve.tensor_tensor(gated[:, c, :], ogn[:, c, :], sg[:, h, c, :], ALU.mult).then_inc(gated_ready, 1)

            def add_attn(h):
                for g in range(2):
                    b = full(dve, ("attn", h, g))
                    s = SUB * h + 2 * g
                    rows = xs[:, s:s + 2, :]
                    dve.tensor_tensor(rows, b[:, :].rearrange("p (s d) -> p s d", d=D), rows,
                                      ALU.add).then_inc(attn_added, 1)
                    dve.wait_ge(attn_added, 2 * h + g + 1)
                    dve.sem_inc(bank_free[6 + g], 1)

            norm_stats(0); normalise(0); split_x(0)
            norm_stats(1); normalise(1)
            dve.wait_ge(tab_in, 16)
            for j in range(FC):
                hidden(0, j)
            low_last(0); split_x(1); hidden(1, 0); hidden(1, 1)
            scale_down(0)
            hidden(1, 2)
            norm_stats(2); normalise(2)
            hidden(1, 3); hidden(1, 4)
            dve.wait_ge(consts, 3)
            shift(0)
            hidden(1, 5); low_last(1)
            scale_delta(0, "w")
            scale_delta(0, "v")
            scale_down(1)
            norm_stats(3); normalise(3)
            scale_delta(0, "k"); scale_delta(0, "r"); 
            scale_delta(0, "g"); bonus_in(0)
            shift(1)
            scale_delta(1, "w"); plane(0, 0); scale_delta(1, "v"); bonus_out(0); plane(0, 4)
            scale_delta(1, "k"); plane(0, 1); plane(0, 5); plane(0, 2); scale_delta(1, "r"); plane(0, 6)
            plane(0, 3); scale_delta(1, "g"); plane(0, 7)
            add_bonus(0); centre(0); bonus_in(1); head_var(0); bonus_out(1); head_scale(0)
            carry_states()
            plane(1, 0); gate_o(0); plane(1, 4); add_attn(0); norm_stats(4); plane(1, 1); normalise(4)
            plane(1, 5); split_x(2)
            plane(1, 2); hidden(2, 0); plane(1, 6); hidden(2, 1); plane(1, 3); plane(1, 7)
            hidden(2, 2); add_bonus(1); hidden(2, 3); centre(1); hidden(2, 4); head_var(1)
            head_scale(1); hidden(2, 5); low_last(2); gate_o(1); add_attn(1); norm_stats(5)
            scale_down(2)
            normalise(5); split_x(3)
            for j in range(FC):
                hidden(3, j)
            low_last(3); scale_down(3)

        @block.scalar
        def _(act):
            def col(c, rows=slice(0, P)):
                return tab[rows, c:c + 1]

            def high_x(u):
                l = u if u < 2 else u + 2
                for c in range(KC):
                    b = full(act, ("xT", l, c))
                    act.activation(xhi[:, u % 2, c, :], b[:, :], ACT.Copy).then_inc(xhi_ready, 1)

            def gate(u, j):
                n = FC * u + j
                if n >= 2:
                    act.wait_ge(hf_ready, n - 1)
                name = ("gate" if j < FULL else "both", u, j)
                b = full(act, name)
                rows, to = (P, 0) if j < FULL else (REM, P - REM)
                act.activation(silu[to:to + rows, n % 2, :], b[0:rows, :], ACT.Silu,
                               scale=col(C_SG + j, slice(0, rows))).then_inc(silu_ready, 1)
                if j < FULL:
                    act.wait_ge(silu_ready, n + 1)
                    act.sem_inc(free(name), 1)

            def high_h(u, j):
                n = FC * u + j
                act.wait_ge(hf_ready, n + 1)
                if u:
                    act.wait_ge(down_done, FC * (u - 1) + j + 1)
                rows = slice(0, P) if j < FULL else slice(P - REM, P)
                act.activation(hhi[rows, j, :], hf[rows, n % 2, :], ACT.Copy).then_inc(hhi_ready, 1)

            def evacuate(name, ready, count, func, dst, src_rows=P, **how):
                b = full(act, name)
                act.activation(dst, b[0:src_rows, :], func, **how).then_inc(ready, 1)
                act.wait_ge(ready, count)
                act.sem_inc(free(name), 1)

            def attn_x(h):
                for c in range(KC):
                    evacuate(("xT", 2 + h, c), xlt_ready, KC * h + c + 1, ACT.Copy,
                             xlt[:, c, TH * h + 1:TH * (h + 1) + 1])

            def low_rank_tanh(h):
                if h:
                    for m in MIXES:
                        full(act, ("rate", h - 1, m, KC - 1))
                evacuate(("z", h), z_ready, 2 * h + 1, ACT.Tanh, zt[:, :])
                evacuate(("zlast", h), z_ready, 2 * h + 2, ACT.Tanh, ztlast, RLO)

            def decay_tanh(h):
                if h:
                    full(act, ("w2", h - 1))
                evacuate(("w", h, 0), tw_ready, h + 1, ACT.Tanh, tw, GLO)

            def values(h):
                if h:
                    act.wait_ge(bonus_v_ready, KC * h)
                    for q in range(4):
                        act.wait_ge(vrep_in[h - 1][q], 64)
                for c in range(KC):
                    evacuate(("v", h, c), v_ready, KC * h + c + 1, ACT.Copy, vt[:, c, :])

            def keys(h):
                evacuate(("k", h, 0), k_ready, h + 1, ACT.Copy, kt[:, h, :])

            def receptance(h):
                evacuate(("r", h, 0), r_ready, h + 1, ACT.Copy, rt[:, h, :])

            def decays(h):
                evacuate(("w2", h), act_seq, h + 1, ACT.Exp, decay[:, h, :], bias=col(C_BW))
                act.activation(decay[:, h, :], decay[:, h, :], ACT.Exp, scale=-1.0).then_inc(decay_ready, 1)

            def gates(h):
                for c in range(KC):
                    evacuate(("g", h, c), sg_ready, KC * h + c + 1, ACT.Silu, sg[:, h, c, :])

            def squares(h):
                act.wait_ge(oc_ready, 2 * (h + 1))
                act.activation(osq[:, :, :], oc[:, :, :], ACT.Square).then_inc(osq_ready, 1)

            def head_std(h):
                act.wait_ge(gvar_ready, h + 1)
                act.activation(gstd[:, :, :], ssum[:, :, :], ACT.Sqrt).then_inc(gstd_ready, 1)

            def norm_affine(h):
                for c in range(KC):
                    evacuate(("ofm", h, c), ogn_ready, KC * h + c + 1, ACT.Identity, ogn[:, c, :],
                             scale=col(C_GNW + c), bias=col(C_GNB + c))

            for q, (lo, hi) in enumerate(((0, 512), (512, 1024), (1024, (2 * FULL + 1) * P))):
                act.wait_ge(wgu_in[q], 16)
                act.activation(wgu_r[:, :, lo:hi], wgu_int[:, :, lo:hi], ACT.Copy,
                               bias=-ZERO_POINT).then_inc(wgu_ready, 1)
                if q == 0:
                    high_x(0)
            act.wait_ge(wd_in, 32)
            act.activation(wd_r[P - REM:P, FULL, :], wd_int[P - REM:P, FULL, :], ACT.Copy,
                           bias=-ZERO_POINT).then_inc(wd_last_ready, 1)
            act.wait_ge(tab_in, 16)
            gate(0, 0); gate(0, 1)
            for j in range(2, FC):
                high_h(0, j - 2); gate(0, j)
            high_h(0, 4); high_x(1); high_h(0, 5)
            gate(1, 0); gate(1, 1)
            for j in range(2, 5):
                high_h(1, j - 2); gate(1, j)
                if j == 4:
                    attn_x(0)
            high_h(1, 3); gate(1, 5); high_h(1, 4)
            low_rank_tanh(0); high_h(1, 5)
            decay_tanh(0); values(0); attn_x(1); keys(0); decays(0); receptance(0)
            low_rank_tanh(1); gates(0)
            decay_tanh(1); values(1); keys(1); decays(1); receptance(1); 
            gates(1); squares(0); head_std(0); norm_affine(0)
            high_x(2)
            gate(2, 0); gate(2, 1)
            for j in range(2, FC):
                high_h(2, j - 2); gate(2, j)
                if j == 4:
                    squares(1); head_std(1)
            high_h(2, 4); high_h(2, 5); norm_affine(1)
            high_x(3)
            gate(3, 0); gate(3, 1)
            for j in range(2, FC):
                high_h(3, j - 2); gate(3, j)
            high_h(3, 4); high_h(3, 5)

        @block.gpsimd
        def _(pool):
            def root(l):
                pool.wait_ge(var_ready, l + 1)
                pool.tensor_tensor(rstd[:, l, :], var_eps[:, l, :], minus_half[:, :], ALU.pow).then_inc(rstd_ready, 1)

            def low_h(u, j):
                n = FC * u + j
                pool.wait_ge(hhi_ready, n + 1)
                if u:
                    pool.wait_ge(down_done, FC * (u - 1) + j + 1)
                pool.tensor_tensor(hlo[:, j, :], hf[:, n % 2, :], hhi[:, j, :].bitcast(fp32), ALU.subtract).then_inc(hlo_ready, 1)

            def add_ffn(u):
                h = u % 2
                for g in range(2):
                    pool.wait_ge(ffn_out_ready, 2 * u + g + 1)
                    rows = xs[:, SUB * h + 2 * g:SUB * h + 2 * g + 2, :]
                    pool.tensor_tensor(rows, rows, ffn_out[:, :].rearrange("p (s d) -> p s d", d=D),
                                       ALU.add).then_inc(residual_ready, 1)

            def add_x(h, m):
                n = 5 * h + MIXES.index(m)
                for c in range(KC):
                    pool.wait_ge(scaled_ready, KC * n + c + 1)
                    pool.tensor_tensor(mix[:, n % 3, c, :], mix[:, n % 3, c, :],
                                       xlt[:, c, TH * h + 1:TH * (h + 1) + 1], ALU.add).then_inc(mix_ready, 1)

            def read_state(h, p):
                pool.wait_ge(scan_ready, PLANES * h + PLANE_ORDER.index(p) + 1)
                pool.wait_ge(r_ready, h + 1)
                pool.tensor_tensor(vrep[:, p, :], rt[:, h, :], state[:, p, 0:TH],
                                   ALU.mult).then_inc(read_ready[1], 1)

            pool.memset(minus_half[:, :], -0.5).then_inc(consts, 1)
            pool.wait_ge(consts, 1)
            root(0)
            pool.memset(xlt[:, :, 0:1], 0.0)
            pool.memset(state[:, :, 0:1], 0.0).then_inc(consts, 1)
            pool.wait_ge(wd_in, 32)
            pool.tensor_scalar(wd_r[:, 0:FULL, :], wd_int[:, 0:FULL, :], -ZERO_POINT, None, ALU.add).then_inc(wd_ready, 1)
            root(1)
            pool.wait_ge(sdn_in, 16)
            pool.tensor_scalar(sdn[:, :], sdn[:, :], 0.5, None, ALU.mult).then_inc(consts, 1)
            for j in range(FULL):
                low_h(0, j)
            low_h(1, 0); add_ffn(0); low_h(1, 1); root(2)
            low_h(1, 2); low_h(1, 3); low_h(1, 4)
            add_x(0, "w"); add_x(0, "v"); add_ffn(1); root(3)
            add_x(0, "k"); add_x(0, "r"); add_x(0, "g")
            add_x(1, "w"); add_x(1, "v"); read_state(0, 4); add_x(1, "k")
            read_state(0, 5); add_x(1, "r"); read_state(0, 6); add_x(1, "g"); read_state(0, 7)
            read_state(1, 4); root(4); read_state(1, 5)
            low_h(2, 0); read_state(1, 6); low_h(2, 1); read_state(1, 7)
            for j in range(2, FULL):
                low_h(2, j)
            root(5)
            add_ffn(2)
            for j in range(FULL):
                low_h(3, j)
            add_ffn(3)

        @block.sync
        def _(sp):
            def load(dst, src, ready):
                sp.dma_start(dst, src).then_inc(ready, 16)

            xv = x[0, :, :].rearrange("(n p) d -> p n d", p=P)
            wguv = wgu.rearrange("(c p) f -> p c f", p=P)
            load(xs[:, 0:SUB, :], xv[:, 0:SUB, :], x_in[0])
            load(wgu_int[:, :, 0:512], wguv[:, :, 0:512], wgu_in[0])
            load(idt[:, :], ident, idt_in)
            load(rept[:, :], rep, idt_in)
            load(tab[:, :], table, tab_in)
            load(wgu_int[:, :, 512:1024], wguv[:, :, 512:1024], wgu_in[1])
            load(wgu_int[:, :, 1024:], wguv[:, :, 1024:], wgu_in[2])
            load(wd_int[:, 0:FULL, :], wd[0:FULL * P, :].rearrange("(c p) d -> p c d", p=P), wd_in)
            load(wd_int[P - REM:P, FULL, :], wd[FULL * P:F, :], wd_in)
            load(xs[:, SUB:2 * SUB, :], xv[:, SUB:2 * SUB, :], x_in[1])
            load(sdn[:, :], sdown.partition_broadcast(P), sdn_in)
            load(wx1s[:, :, :], wx1.rearrange("(c p) f -> p c f", p=P), wz_in)
            load(wx2s[:, :], wx2[0:P, :], wz_in)
            load(wx2last[P - RLO:P, :], wx2[P:MIX * RLO, :], wz_in)
            for dst, src in ((ww1s, ww1), (wvs, wv), (wks, wk), (wrs, wr), (wgs, wg), (wos, wo)):
                load(dst[:, :, :], src.rearrange("(c p) f -> p c f", p=P), wp_in)
            load(ww2s[:, :], ww2, wp_in)
            for h in range(HALVES):
                sp.wait_ge(v_ready, KC * (h + 1))
                for q in range(4):
                    if h:
                        full(sp, ("o", h - 1, 0))
                        full(sp, ("o", h - 1, 1))
                    for k in range(HQK):
                        sp.dma_start(vrep[k * NH:(k + 1) * NH, q::4, :],
                                     vt[q * NH:(q + 1) * NH, :, :]).then_inc(vrep_in[h][q], 16)
            outv = out[0, :, :].rearrange("(n p) d -> p n d", p=P)
            for h in range(HALVES):
                for g in range(2):
                    sp.wait_ge(residual_ready, 2 * (2 + h) + g + 1)
                    s = SUB * h + 2 * g
                    sp.dma_start(outv[:, s:s + 2, :], xs[:, s:s + 2, :]).then_inc(stored, 16)
            sp.wait_ge(stored, 64)


def kernel(**inputs):
    import numpy as _np
    import concourse.bacc as _bacc
    from concourse import mybir as _mybir
    from concourse.bass_utils import run_bass_kernel_spmd as _run

    a = {n.replace("L0_attn_", "").replace("L0_ffn_", ""): _np.asarray(v) for n, v in inputs.items()}

    def by_key(w):
        return w.reshape(-1, NH, HQK).transpose(0, 2, 1).reshape(-1, NH * HQK)

    def by_value(w):
        return w.reshape(-1, NH, HV).transpose(0, 2, 1).reshape(-1, NH * HV)

    gate, up = a["wq_gate"].T, a["wq_up"].T
    parts = [w[:, j * P:(j + 1) * P] for j in range(FULL) for w in (gate, up)]
    parts += [gate[:, FULL * P:], up[:, FULL * P:]]

    table = _np.zeros((P, C_ALL), _np.float32)
    table[:, C_SG:C_SG + FULL] = a["s_gate"][:FULL * P].reshape(FULL, P).T
    table[:REM, C_SG + FULL] = a["s_gate"][FULL * P:]
    table[:, C_SU:C_SU + FULL] = a["s_up"][:FULL * P].reshape(FULL, P).T
    table[P - REM:, C_SU + FULL] = a["s_up"][FULL * P:]
    table[:, C_MU:C_MU + 2] = a["mu_x"].reshape(KC, P).T
    table[:, C_BW] = by_key(a["bw"])[0]
    table[:, C_BONUS] = by_key(a["bonus"].reshape(-1))[0]
    table[:, C_GNW:C_GNW + 2] = _np.repeat(a["gn_w"], NH).reshape(KC, P).T
    table[:, C_GNB:C_GNB + 2] = _np.repeat(a["gn_b"], NH).reshape(KC, P).T

    arrays = {
        "x": a["hidden_states"], "wgu": _np.concatenate(parts, 1), "wd": a["wq_down"].T, "table": table,
        "sdown": a["s_down"], "wx1": a["Wx1"], "wx2": a["Wx2"].reshape(MIX * RLO, D),
        "wr": by_key(a["Wr"]), "wk": by_key(a["Wk"]), "wv": by_value(a["Wv"]), "wg": by_value(a["Wg"]),
        "ww1": a["Ww1"], "ww2": by_key(a["Ww2"]),
        "wo": a["Wo"].reshape(NH, HV, D).transpose(1, 0, 2).reshape(NH * HV, D),
        "ident": _np.eye(P, dtype=_np.float32),
        "rep": _np.tile(_np.eye(NH, dtype=_np.float32), (4, 4)),
    }
    nc = _bacc.Bacc("TRN2", target_bir_lowering=False, num_devices=1)
    arrays = {n: _np.ascontiguousarray(v) for n, v in arrays.items()}
    args = [nc.dram_tensor(n, v.shape, _mybir.dt.from_np(v.dtype), kind="ExternalInput").ap()
            for n, v in arrays.items()]
    out = nc.dram_tensor("out", (1, T, D), _mybir.dt.float32, kind="ExternalOutput").ap()
    macaron(nc, *args, out)
    r = _run(nc, [arrays], core_ids=[0])
    return r.results[0]["out"]
```

```python
from contextlib import ExitStack

import concourse.bass as bass
import numpy as np
from concourse import mybir

T, D, F = 1024, 256, 704
P = 128
NQ = 4
TQ = T // NQ
SUB = TQ // P
KC = D // P
FULL = F // P
REM = F - FULL * P
FC = FULL + 1
WGU = (2 * FULL + 1) * P
NH, HQK, HV = 32, 4, 8
PAIRS = HV // 2
RLO, GLO, MIX = 32, 64, 5
EPS = 1e-5
ZERO_POINT = 128.0
OWN_SIGNAL = ("o", "down")
RING = 3
MRING = 4

C_SG, C_SU, C_MU, C_BW, C_BONUS, C_GNW, C_GNB = 0, FC, 2 * FC, 2 * FC + 2, 2 * FC + 3, 2 * FC + 4, 2 * FC + 6
C_ALL = 2 * FC + 8

MIXES = ["w", "v", "k", "r", "g"]
INDEX = {"r": 0, "w": 1, "k": 2, "v": 3, "g": 4}
POOL_PAIRS = (2, 3)
WGU_PARTS = ((0, 256), (256, 768), (768, WGU))


def macaron(nc, x, wgu, wd, table, sdown, wx1, wx2, wr, wk, wv, wg, ww1, ww2, wo, ident, rep, out):
    fp32, fp32r, int32 = mybir.dt.float32, mybir.dt.float32r, mybir.dt.int32
    ALU, ACT, AX = mybir.AluOpType, mybir.ActivationFunctionType, mybir.AxisListType
    ctx = ExitStack()
    with ctx:
        def sb(name, shape, dt=fp32):
            return ctx.enter_context(nc.sbuf_tensor(name, shape, dt))

        def sem(name):
            return ctx.enter_context(nc.semaphore(name))

        xs = sb("xs", [P, T // P, D])
        tab = sb("tab", [P, C_ALL])
        sdn = sb("sdn", [P, D])
        idt = sb("idt", [P, P])
        rept = sb("rept", [P, P])
        minus_half = sb("minus_half", [P, SUB])
        wgu_int = sb("wgu_int", [P, KC, WGU], int32)
        wgu_r = sb("wgu_r", [P, KC, WGU], fp32r)
        wd_int = sb("wd_int", [P, FC, D], int32)
        wd_r = sb("wd_r", [P, FC, D], fp32r)
        wx1s = sb("wx1s", [P, KC, MIX * RLO])
        wx2s = sb("wx2s", [P, D])
        wx2last = sb("wx2last", [RLO, D])
        wrs = sb("wrs", [P, KC, P])
        wks = sb("wks", [P, KC, P])
        wvs = sb("wvs", [P, KC, D])
        wgs = sb("wgs", [P, KC, D])
        ww1s = sb("ww1s", [P, KC, GLO])
        ww2s = sb("ww2s", [GLO, P])
        wos = sb("wos", [P, KC, D])

        stats = sb("stats", [P, 3 * NQ, SUB, 6])
        mv = sb("mv", [P, 3 * NQ, SUB, 2])
        var_eps = sb("var_eps", [P, 3 * NQ, SUB])
        rstd = sb("rstd", [P, 3 * NQ, SUB])
        xn = sb("xn", [P, 2, SUB, D])

        xhi = sb("xhi", [P, 2, KC, TQ], fp32r)
        xlo = sb("xlo", [P, 2, KC, TQ], fp32r)
        silu = sb("silu", [P, RING, TQ])
        hf = sb("hf", [P, RING, TQ])
        hhi = sb("hhi", [P, FC, TQ], fp32r)
        hlo = sb("hlo", [P, FC, TQ], fp32r)
        ffn_out = sb("ffn_out", [P, 2, SUB, D])

        xlt = sb("xlt", [P, KC, T + 1])
        delta = sb("delta", [P, 2, KC, TQ])
        xmu = sb("xmu", [P, 2, KC, TQ])
        zt = sb("zt", [P, 2, TQ])
        ztlast = sb("ztlast", [RLO, 2, TQ])
        mix = sb("mix", [P, MRING, KC, TQ])
        tw = sb("tw", [GLO, 2, TQ])
        expw = sb("expw", [P, TQ])
        decay = sb("decay", [P, T])
        vt = sb("vt", [P, 2, KC, TQ])
        kt = sb("kt", [P, 2, TQ])
        rt = sb("rt", [P, T])
        sg = sb("sg", [P, NQ, KC, TQ])
        rbk = sb("rbk", [P, 2, TQ])
        bonus_v = sb("bonus_v", [P, 2, KC, TQ])
        vrep = sb("vrep", [P, 2, PAIRS, 2, TQ])
        state = sb("state", [P, HV, T + 1])
        ot = sb("ot", [P, KC, TQ])
        vsum = sb("vsum", [P, SUB, NH])
        oc = sb("oc", [P, SUB, D])
        osq = sb("osq", [P, SUB, D])
        ssum = sb("ssum", [P, SUB, NH])
        gstd = sb("gstd", [P, SUB, NH])
        ogn = sb("ogn", [P, KC, TQ])
        v_dram = nc.dram_tensor("v_dram", (NQ, P, KC * TQ), fp32, kind="Internal").ap()

        bank = [ctx.enter_context(nc.psum_tensor(f"bank{b}", [P, 2 * TQ], fp32)) for b in range(8)]
        bank_full = [sem(f"bank_full{b}") for b in range(8)]

        x_in = [sem(f"x_in{h}") for h in range(NQ)]
        wgu_in = [sem(f"wgu_in{q}") for q in range(len(WGU_PARTS))]
        wd_in = sem("wd_in")
        tab_in = sem("tab_in")
        sdn_in = sem("sdn_in")
        idt_in = sem("idt_in")
        wz_in = sem("wz_in")
        wp_in = sem("wp_in")
        stored = sem("stored")
        v_out = [sem(f"v_out{h}") for h in range(NQ)]
        vrep_in = [sem(f"vrep_in{h}") for h in range(NQ)]
        wgu_ready = sem("wgu_ready")
        wd_ready = sem("wd_ready")
        wd_last_ready = sem("wd_last_ready")
        consts = sem("consts")
        dve_seq = sem("dve_seq")
        var_ready = sem("var_ready")
        rstd_ready = sem("rstd_ready")
        xn_ready = sem("xn_ready")
        xhi_ready = sem("xhi_ready")
        xlo_ready = sem("xlo_ready")
        silu_ready = sem("silu_ready")
        hf_ready = sem("hf_ready")
        hhi_ready = sem("hhi_ready")
        hlo_ready = sem("hlo_ready")
        hlo_last_ready = sem("hlo_last_ready")
        down_done = sem("down_done")
        ffn_out_ready = sem("ffn_out_ready")
        residual_ready = sem("residual_ready")
        attn_added = sem("attn_added")
        xlt_ready = sem("xlt_ready")
        xmu_ready = sem("xmu_ready")
        z_ready = sem("z_ready")
        scaled_ready = sem("scaled_ready")
        mix_ready = sem("mix_ready")
        tw_ready = sem("tw_ready")
        expw_ready = sem("expw_ready")
        decay_ready = sem("decay_ready")
        v_ready = sem("v_ready")
        k_ready = sem("k_ready")
        r_ready = sem("r_ready")
        sg_ready = sem("sg_ready")
        rbk_ready = sem("rbk_ready")
        bonus_v_ready = sem("bonus_v_ready")
        scan_ready = sem("scan_ready")
        read_ready = [sem("read_ready_dve"), sem("read_ready_pool")]
        key_summed = sem("key_summed")
        ot_ready = sem("ot_ready")
        oc_ready = sem("oc_ready")
        osq_ready = sem("osq_ready")
        gvar_ready = sem("gvar_ready")
        gstd_ready = sem("gstd_ready")
        on_ready = sem("on_ready")
        ogn_ready = sem("ogn_ready")
        gated_ready = sem("gated_ready")

        def norm_use(l):
            return l if l < NQ else l - NQ if l >= 2 * NQ else None

        def mix_number(h, m):
            return MIX * h + MIXES.index(m)

        def read_out(name):
            kind, i = name[0], name[1]
            if kind == "xT":
                u = norm_use(i)
                return (xlt_ready, i - NQ + 1) if u is None else (xlo_ready, u + 1)
            if kind == "gate_up":
                return hf_ready, FC * i + name[2] + 1
            if kind == "rate":
                return scaled_ready, mix_number(i, name[2]) + 1
            ready, per = {"down": (ffn_out_ready, 1), "z": (z_ready, 2), "w": (tw_ready, 1), "v": (v_ready, 1),
                          "k": (k_ready, 1), "r": (r_ready, 1), "g": (sg_ready, 1), "w2": (expw_ready, 1),
                          "bonus": (bonus_v_ready, 1), "o": (ot_ready, 1), "otm": (oc_ready, 1),
                          "ofm": (ogn_ready, 2), "attn": (attn_added, 1)}[kind]
            return ready, per * (i + 1)

        fills = {}
        filled = [[] for _ in range(8)]

        def full(eng, name):
            b, n = fills[name]
            eng.wait_ge(bank_full[b], n + 1)
            return bank[b]

        def halves(tile):
            return tile.rearrange("p (a t) -> p a t", a=2)

        block = ctx.enter_context(nc.Block())

        @block.tensor
        def _(pe):
            def take(b, name):
                if filled[b]:
                    ready, value = read_out(filled[b][-1])
                    pe.wait_ge(ready, value)
                fills[name] = (b, sum(other[0] not in OWN_SIGNAL for other in filled[b]))
                filled[b].append(name)
                return bank[b]

            turns = {0: [0, 4], 4: [0, 2], 6: [0, 2]}

            def take_next(group, name):
                turn = turns[group]
                turn[0] += 1
                return take(group + (turn[0] - 1) % turn[1], name)

            def done(ins, name):
                ins.then_inc(bank_full[fills[name][0]], 1)

            def transpose_x(l):
                pe.wait_ge(xn_ready, l + 1)
                b = take_next(6, ("xT", l))
                for c in range(KC):
                    for s in range(SUB):
                        ins = pe.transpose(b[:, c * TQ + s * P:c * TQ + (s + 1) * P],
                                           xn[:, l % 2, s, c * P:(c + 1) * P], idt[:, :])
                done(ins, ("xT", l))

            def gate_up(u, j):
                if u == 0:
                    pe.wait_ge(wgu_ready, 1 + sum(2 * j * P >= lo for lo, _ in WGU_PARTS[1:]))
                b = take_next(0, ("gate_up", u, j))
                for a in range(2 if j < FULL else 1):
                    w = (2 * j + a) * P
                    for n, part in enumerate((xhi, xlo)):
                        if j == 0 and a == 0:
                            pe.wait_ge((xhi_ready, xlo_ready)[n], u + 1)
                        for c in range(KC):
                            ins = pe.matmul(b[:, a * TQ:(a + 1) * TQ], wgu_r[:, c, w:w + P], part[:, u % 2, c, :],
                                            start=(n == 0 and c == 0), stop=(n == 1 and c == KC - 1))
                done(ins, ("gate_up", u, j))

            def down(u, j):
                if j == 0:
                    if u == 0:
                        pe.wait_ge(wd_ready, 1)
                    take_next(4, ("down", u))
                b = bank[fills["down", u][0]]
                lo = 0 if j < FULL else P - REM
                if u == 0 and j == FULL:
                    pe.wait_ge(wd_last_ready, 1)
                for n, part in enumerate((hhi, hlo)):
                    if n == 0:
                        pe.wait_ge(hhi_ready, FC * u + j + 1)
                    elif j < FULL:
                        pe.wait_ge(hlo_ready, FULL * u + j + 1)
                    else:
                        pe.wait_ge(hlo_last_ready, u + 1)
                    for s in range(SUB):
                        ins = pe.matmul(b[:, s * D:(s + 1) * D], part[lo:P, j, s * P:(s + 1) * P], wd_r[lo:P, j, :],
                                        start=(j == 0 and n == 0 and s == 0), stop=(j == FC - 1 and n == 1),
                                        skip_group_check=True)
                ins.then_inc(down_done, 1)

            def low_rank(h):
                if h == 0:
                    pe.wait_ge(wz_in, 48)
                pe.wait_ge(xmu_ready, KC * (h + 1))
                b = take_next(0, ("z", h))
                for a, (lo, hi) in enumerate(((0, P), (P, MIX * RLO))):
                    for c in range(KC):
                        ins = pe.matmul(b[0:hi - lo, a * TQ:(a + 1) * TQ], wx1s[:, c, lo:hi], xmu[:, h % 2, c, :],
                                        start=(c == 0), stop=(c == KC - 1))
                done(ins, ("z", h))

            def mix_rate(h, m):
                i = INDEX[m]
                pe.wait_ge(z_ready, 2 * h + (1 if i < 4 else 2))
                b = take_next(0, ("rate", h, m))
                for c in range(KC):
                    if i < 4:
                        w, z = wx2s[i * RLO:(i + 1) * RLO, c * P:(c + 1) * P], zt[i * RLO:(i + 1) * RLO, h % 2, :]
                    else:
                        w, z = wx2last[:, c * P:(c + 1) * P], ztlast[:, h % 2, :]
                    ins = pe.matmul(b[:, c * TQ:(c + 1) * TQ], w, z, start=True, stop=True)
                done(ins, ("rate", h, m))

            def project(h, m):
                w, outs = {"w": (ww1s, (GLO,)), "v": (wvs, (P, P)), "k": (wks, (P,)),
                           "r": (wrs, (P,)), "g": (wgs, (P, P))}[m]
                n = mix_number(h, m)
                if n == 0:
                    pe.wait_ge(wp_in, 112)
                pe.wait_ge(mix_ready, n + 1)
                b = take_next(0, (m, h))
                for o, rows in enumerate(outs):
                    for c in range(KC):
                        ins = pe.matmul(b[0:rows, o * TQ:(o + 1) * TQ], w[:, c, o * P:o * P + rows],
                                        mix[:, n % MRING, c, :], start=(c == 0), stop=(c == KC - 1))
                done(ins, (m, h))

            def decay_logit(h):
                pe.wait_ge(tw_ready, h + 1)
                b = take_next(0, ("w2", h))
                done(pe.matmul(b[:, 0:TQ], ww2s[:, :], tw[:, h % 2, :], start=True, stop=True), ("w2", h))

            def bonus_sum(h):
                pe.wait_ge(rbk_ready, h + 1)
                b = take_next(0, ("bonus", h))
                done(pe.matmul(b[:, 0:TQ], rept[:, :], rbk[:, h % 2, :], start=True, stop=True), ("bonus", h))

            def key_sum(h, q):
                if q == 0:
                    take_next(6, ("o", h))
                b = bank[fills["o", h][0]]
                who = int(q in POOL_PAIRS)
                pe.wait_ge(read_ready[who], 2 * h + q % 2 + 1)
                pe.matmul(b[q * NH:(q + 1) * NH, :], rept[:, 0:NH], vrep[:, h % 2, q, :, :],
                          start=True, stop=True).then_inc(key_summed, 1)

            def o_token_major(h):
                pe.wait_ge(ot_ready, h + 1)
                b = take_next(6, ("otm", h))
                for s in range(SUB):
                    for c in range(KC):
                        ins = pe.transpose(b[:, s * D + c * P:s * D + (c + 1) * P], ot[:, c, s * P:(s + 1) * P],
                                           idt[:, :])
                done(ins, ("otm", h))

            def o_feature_major(h):
                pe.wait_ge(on_ready, h + 1)
                b = take_next(6, ("ofm", h))
                for c in range(KC):
                    for s in range(SUB):
                        ins = pe.transpose(b[:, c * TQ + s * P:c * TQ + (s + 1) * P], oc[:, s, c * P:(c + 1) * P],
                                           idt[:, :])
                done(ins, ("ofm", h))

            def output(h):
                pe.wait_ge(gated_ready, h + 1)
                b = take_next(6, ("attn", h))
                for s in range(SUB):
                    for c in range(KC):
                        ins = pe.matmul(b[:, s * D:(s + 1) * D], ogn[:, c, s * P:(s + 1) * P], wos[:, c, :],
                                        start=(c == 0), stop=(c == KC - 1))
                done(ins, ("attn", h))

            pe.wait_ge(idt_in, 32)
            transpose_x(0); transpose_x(1); gate_up(0, 0); transpose_x(2); gate_up(0, 1); gate_up(0, 2)
            gate_up(0, 3); gate_up(0, 4); down(0, 0); gate_up(0, 5); down(0, 1); transpose_x(3); down(0, 2)
            down(0, 3); gate_up(1, 0); down(0, 4); down(0, 5); gate_up(1, 1); gate_up(1, 2); gate_up(1, 3)
            down(1, 0); gate_up(1, 4); down(1, 1); gate_up(1, 5); transpose_x(4); gate_up(2, 0); down(1, 2)
            gate_up(2, 1); gate_up(2, 2); low_rank(0); gate_up(2, 3); down(1, 3); mix_rate(0, "w"); mix_rate(0, "v")
            gate_up(2, 4); mix_rate(0, "k"); project(0, "w"); mix_rate(0, "r"); project(0, "v"); mix_rate(0, "g")
            gate_up(2, 5); gate_up(3, 0); project(0, "k"); project(0, "r"); project(0, "g"); down(1, 4); down(1, 5)
            down(2, 0); down(2, 1); down(2, 2); down(2, 3); down(2, 4); down(2, 5); bonus_sum(0); decay_logit(0)
            gate_up(3, 1); transpose_x(5); gate_up(3, 2); gate_up(3, 3); gate_up(3, 4); down(3, 0); key_sum(0, 0)
            transpose_x(6); gate_up(3, 5); low_rank(1); down(3, 1); key_sum(0, 1); mix_rate(1, "w")
            mix_rate(1, "v"); down(3, 2); down(3, 3); key_sum(0, 2); down(3, 4); project(1, "w"); down(3, 5)
            project(1, "v"); key_sum(0, 3); decay_logit(1); mix_rate(1, "k"); mix_rate(1, "r"); mix_rate(1, "g")
            o_token_major(0); transpose_x(7); project(1, "k"); project(1, "r"); low_rank(2); project(1, "g")
            mix_rate(2, "w"); mix_rate(2, "v"); mix_rate(2, "k"); mix_rate(2, "r"); key_sum(1, 0); key_sum(1, 1)
            key_sum(1, 2); mix_rate(2, "g"); bonus_sum(1); project(2, "w"); key_sum(1, 3); project(2, "v")
            o_token_major(1); o_feature_major(0); decay_logit(2); project(2, "k"); low_rank(3); project(2, "r")
            output(0); mix_rate(3, "w"); project(2, "g"); mix_rate(3, "v"); project(3, "w"); key_sum(2, 0)
            mix_rate(3, "k"); bonus_sum(2); key_sum(2, 1); mix_rate(3, "r"); project(3, "v"); project(3, "k")
            o_feature_major(1); project(3, "r"); mix_rate(3, "g"); decay_logit(3); key_sum(2, 2); key_sum(2, 3)
            bonus_sum(3); o_token_major(2); transpose_x(8); project(3, "g"); output(1); gate_up(4, 0); gate_up(4, 1)
            gate_up(4, 2); gate_up(4, 3); gate_up(4, 4); transpose_x(9); gate_up(4, 5); down(4, 0); down(4, 1)
            key_sum(3, 0); key_sum(3, 1); key_sum(3, 2); key_sum(3, 3); o_feature_major(2); down(4, 2)
            o_token_major(3); gate_up(5, 0); output(2); gate_up(5, 1); down(4, 3); gate_up(5, 2); gate_up(5, 3)
            down(4, 4); down(4, 5); gate_up(5, 4); o_feature_major(3); down(5, 0); transpose_x(10); gate_up(5, 5)
            output(3); gate_up(6, 0); down(5, 1); gate_up(6, 1); gate_up(6, 2); gate_up(6, 3); gate_up(6, 4)
            down(5, 2); transpose_x(11); down(5, 3); down(5, 4); gate_up(6, 5); down(5, 5); down(6, 0); down(6, 1)
            gate_up(7, 0); gate_up(7, 1); down(6, 2); gate_up(7, 2); gate_up(7, 3); down(6, 3); gate_up(7, 4)
            down(6, 4); down(6, 5); down(7, 0); gate_up(7, 5); down(7, 1); down(7, 2); down(7, 3); down(7, 4)
            down(7, 5)

        @block.vector
        def _(dve):
            steps = [0]

            def step(ins):
                steps[0] += 1
                ins.then_inc(dve_seq, 1)

            def settle():
                dve.wait_ge(dve_seq, steps[0])

            def col(c, rows=slice(0, P)):
                return tab[rows, c:c + 1]

            def quarter(h):
                return slice(h * TQ, (h + 1) * TQ)

            def rows_of(h):
                return xs[:, SUB * h:SUB * (h + 1), :]

            def norm_stats(l):
                h = l % NQ
                if l < NQ:
                    dve.wait_ge(x_in[h], 16)
                elif l < 2 * NQ:
                    dve.wait_ge(residual_ready, h + 1)
                else:
                    dve.wait_ge(attn_added, h + 1)
                for s in range(SUB):
                    step(dve.bn_stats(stats[:, l, s, :], xs[:, SUB * h + s, :]))
                settle()
                for s in range(SUB):
                    step(dve.bn_aggr(mv[:, l, s, :], stats[:, l, s, :]))
                settle()
                dve.tensor_scalar(var_eps[:, l, :], mv[:, l, :, 1], EPS, None, ALU.add).then_inc(var_ready, 1)

            def normalise(l):
                h = l % NQ
                dve.wait_ge(rstd_ready, l + 1)
                if l >= 2:
                    full(dve, ("xT", l - 2))
                for s in range(SUB):
                    ins = dve.tensor_scalar(xn[:, l % 2, s, :], xs[:, SUB * h + s, :], mv[:, l, s, 0:1],
                                            rstd[:, l, s:s + 1], ALU.subtract, ALU.mult)
                ins.then_inc(xn_ready, 1)

            def split_x(u):
                l = u if u < NQ else u + NQ
                dve.wait_ge(xhi_ready, u + 1)
                if u >= 2:
                    full(dve, ("gate_up", u - 2, FC - 1))
                b = full(dve, ("xT", l))
                dve.tensor_tensor(xlo[:, u % 2, :, :], halves(b[:, :]), xhi[:, u % 2, :, :].bitcast(fp32),
                                  ALU.subtract).then_inc(xlo_ready, 1)

            def hidden(u, j):
                n = FC * u + j
                if n == 0:
                    dve.wait_ge(tab_in, 16)
                dve.wait_ge(silu_ready, n + 1)
                if n >= RING:
                    v, i = divmod(n - RING, FC)
                    dve.wait_ge(hhi_ready, n - RING + 1)
                    if i < FULL:
                        dve.wait_ge(hlo_ready, FULL * v + i + 1)
                    else:
                        dve.wait_ge(hlo_last_ready, v + 1)
                b = full(dve, ("gate_up", u, j))
                rows, at = (slice(0, P), TQ) if j < FULL else (slice(P - REM, P), 0)
                dve.scalar_tensor_tensor(hf[rows, n % RING, :], b[rows, at:at + TQ], col(C_SU + j, rows),
                                         silu[rows, n % RING, :], ALU.mult, ALU.mult).then_inc(hf_ready, 1)

            def low_last(u):
                n = FC * u + FULL
                dve.wait_ge(hhi_ready, n + 1)
                if u:
                    dve.wait_ge(down_done, FC * u)
                rows = slice(P - REM, P)
                dve.tensor_tensor(hlo[rows, FULL, :], hf[rows, n % RING, :], hhi[rows, FULL, :].bitcast(fp32),
                                  ALU.subtract).then_inc(hlo_last_ready, 1)

            def scale_down(u):
                dve.wait_ge(down_done, FC * (u + 1))
                if u == 0:
                    dve.wait_ge(consts, 3)
                if u >= 2:
                    dve.wait_ge(residual_ready, u - 1)
                b = bank[fills["down", u][0]]
                dve.tensor_tensor(ffn_out[:, u % 2, :, :], halves(b[:, :]),
                                  sdn[:, :].unsqueeze(1).to_broadcast([P, SUB, D]), ALU.mult).then_inc(ffn_out_ready, 1)

            def shift(h):
                if h == 0:
                    dve.wait_ge(consts, 2)
                dve.wait_ge(xlt_ready, h + 1)
                at = TQ * h
                step(dve.tensor_tensor(delta[:, h % 2, :, :], xlt[:, :, at:at + TQ], xlt[:, :, at + 1:at + TQ + 1],
                                       ALU.subtract))
                settle()
                if h >= 2:
                    full(dve, ("z", h - 2))
                for c in range(KC):
                    dve.scalar_tensor_tensor(xmu[:, h % 2, c, :], delta[:, h % 2, c, :], col(C_MU + c),
                                             xlt[:, c, at + 1:at + TQ + 1], ALU.mult, ALU.add).then_inc(xmu_ready, 1)

            def scale_delta(h, m):
                n = mix_number(h, m)
                if n >= MRING:
                    full(dve, (MIXES[(n - MRING) % MIX], (n - MRING) // MIX))
                b = full(dve, ("rate", h, m))
                dve.tensor_tensor(mix[:, n % MRING, :, :], halves(b[:, :]), delta[:, h % 2, :, :],
                                  ALU.mult).then_inc(scaled_ready, 1)

            def bonus_in(h):
                dve.wait_ge(r_ready, h + 1)
                dve.wait_ge(k_ready, h + 1)
                if h >= 2:
                    full(dve, ("bonus", h - 2))
                dve.scalar_tensor_tensor(rbk[:, h % 2, :], rt[:, quarter(h)], col(C_BONUS), kt[:, h % 2, :],
                                         ALU.mult, ALU.mult).then_inc(rbk_ready, 1)

            def bonus_out(h):
                b = full(dve, ("bonus", h))
                dve.wait_ge(v_ready, h + 1)
                dve.tensor_tensor(bonus_v[:, h % 2, :, :], b[:, 0:TQ].unsqueeze(1).to_broadcast([P, KC, TQ]),
                                  vt[:, h % 2, :, :], ALU.mult).then_inc(bonus_v_ready, 1)

            def plane(h, q):
                dve.wait_ge(vrep_in[h], 16 * HQK)
                dve.wait_ge(decay_ready, h + 1)
                dve.wait_ge(k_ready, h + 1)
                kv = vrep[:, h % 2, q, :, :]
                step(dve.tensor_tensor(kv, kt[:, h % 2, :].unsqueeze(1).to_broadcast([P, 2, TQ]), kv, ALU.mult))
                settle()
                at = TQ * h
                for a in range(2):
                    p = 2 * q + a
                    dve.tensor_tensor_scan(state[:, p, at + 1:at + TQ + 1], decay[:, quarter(h)],
                                           vrep[:, h % 2, q, a, :], state[:, p, at:at + 1],
                                           ALU.mult, ALU.add).then_inc(scan_ready, 1)
                if q not in POOL_PAIRS:
                    dve.wait_ge(scan_ready, HV * h + 2 * q + 2)
                    dve.wait_ge(r_ready, h + 1)
                    dve.tensor_tensor(kv, rt[:, quarter(h)].unsqueeze(1).to_broadcast([P, 2, TQ]),
                                      state[:, 2 * q:2 * q + 2, at:at + TQ], ALU.mult).then_inc(read_ready[0], 1)

            def add_bonus(h):
                dve.wait_ge(key_summed, PAIRS * (h + 1))
                dve.wait_ge(bonus_v_ready, h + 1)
                b = bank[fills["o", h][0]]
                dve.tensor_tensor(ot[:, :, :], halves(b[:, :]), bonus_v[:, h % 2, :, :], ALU.add).then_inc(ot_ready, 1)

            def by_head(tile):
                return tile.rearrange("p s (v n) -> p s v n", n=NH)

            def per_head(tile):
                return tile.unsqueeze(2).to_broadcast([P, SUB, HV, NH])

            def centre(h):
                b = full(dve, ("otm", h))
                step(dve.tensor_reduce(vsum[:, :, :], b[:, :].rearrange("p (s v n) -> p s n v", s=SUB, n=NH),
                                       AX.X, ALU.add))
                settle()
                step(dve.tensor_scalar(vsum[:, :, :], vsum[:, :, :], 1.0 / HV, None, ALU.mult))
                settle()
                if h:
                    full(dve, ("ofm", h - 1))
                dve.tensor_tensor(by_head(oc[:, :, :]), by_head(halves(b[:, :])), per_head(vsum[:, :, :]),
                                  ALU.subtract).then_inc(oc_ready, 1)

            def head_var(h):
                dve.wait_ge(osq_ready, h + 1)
                step(dve.tensor_reduce(ssum[:, :, :], osq[:, :, :].rearrange("p s (v n) -> p s n v", n=NH),
                                       AX.X, ALU.add))
                settle()
                dve.tensor_scalar(ssum[:, :, :], ssum[:, :, :], 1.0 / HV, EPS, ALU.mult, ALU.add).then_inc(gvar_ready, 1)

            def head_scale(h):
                dve.wait_ge(gstd_ready, h + 1)
                step(dve.reciprocal(gstd[:, :, :], gstd[:, :, :]))
                settle()
                dve.tensor_tensor(by_head(oc[:, :, :]), by_head(oc[:, :, :]), per_head(gstd[:, :, :]),
                                  ALU.mult).then_inc(on_ready, 1)

            def gate_o(h):
                dve.wait_ge(ogn_ready, KC * (h + 1))
                dve.wait_ge(sg_ready, h + 1)
                dve.tensor_tensor(ogn[:, :, :], ogn[:, :, :], sg[:, h, :, :], ALU.mult).then_inc(gated_ready, 1)

            def add_attn(h):
                b = full(dve, ("attn", h))
                dve.tensor_tensor(rows_of(h), halves(b[:, :]), rows_of(h), ALU.add).then_inc(attn_added, 1)

            norm_stats(0); norm_stats(1); normalise(0); norm_stats(2); normalise(1); normalise(2); split_x(0)
            split_x(1); norm_stats(3); hidden(0, 0); hidden(0, 1); normalise(3); hidden(0, 2); hidden(0, 3)
            hidden(0, 4); hidden(0, 5); split_x(2); low_last(0); hidden(1, 0); scale_down(0); hidden(1, 1)
            norm_stats(4); hidden(1, 2); hidden(1, 3); normalise(4); hidden(1, 4); hidden(1, 5); shift(0)
            low_last(1); split_x(3); hidden(2, 0); hidden(2, 1); hidden(2, 2); hidden(2, 3); scale_delta(0, "w")
            scale_delta(0, "v"); hidden(2, 4); scale_delta(0, "k"); scale_delta(0, "r"); scale_delta(0, "g")
            hidden(2, 5); bonus_in(0); scale_down(1); low_last(2); hidden(3, 0); norm_stats(5); scale_down(2)
            normalise(5); bonus_out(0); norm_stats(6); plane(0, 0); normalise(6); hidden(3, 1); shift(1)
            hidden(3, 2); plane(0, 1); hidden(3, 3); hidden(3, 4); plane(0, 2); scale_delta(1, "w"); hidden(3, 5)
            scale_delta(1, "v"); low_last(3); plane(0, 3); scale_down(3); norm_stats(7); add_bonus(0)
            scale_delta(1, "k"); scale_delta(1, "r"); normalise(7); scale_delta(1, "g"); shift(2); centre(0)
            plane(1, 0); plane(1, 1); plane(1, 2); plane(1, 3); bonus_in(1); scale_delta(2, "w")
            scale_delta(2, "v"); scale_delta(2, "k"); head_var(0); bonus_out(1); scale_delta(2, "r"); add_bonus(1)
            head_scale(0); scale_delta(2, "g"); shift(3); gate_o(0); centre(1); head_var(1); bonus_in(2)
            add_attn(0); scale_delta(3, "w"); plane(2, 0); scale_delta(3, "v"); plane(2, 1); bonus_out(2)
            scale_delta(3, "k"); head_scale(1); scale_delta(3, "r"); norm_stats(8); plane(2, 2); plane(2, 3)
            scale_delta(3, "g"); gate_o(1); normalise(8); bonus_in(3); add_bonus(2); bonus_out(3); centre(2)
            plane(3, 0); split_x(4); add_attn(1); norm_stats(9); hidden(4, 0); head_var(2); hidden(4, 1)
            normalise(9); plane(3, 1); plane(3, 2); plane(3, 3); head_scale(2); hidden(4, 2); split_x(5)
            add_bonus(3); hidden(4, 3); hidden(4, 4); gate_o(2); centre(3); hidden(4, 5); add_attn(2); head_var(3)
            low_last(4); norm_stats(10); hidden(5, 0); head_scale(3); scale_down(4); normalise(10); hidden(5, 1)
            gate_o(3); hidden(5, 2); split_x(6); hidden(5, 3); hidden(5, 4); add_attn(3); norm_stats(11)
            hidden(5, 5); hidden(6, 0); low_last(5); normalise(11); hidden(6, 1); hidden(6, 2); hidden(6, 3)
            hidden(6, 4); split_x(7); hidden(6, 5); scale_down(5); low_last(6); hidden(7, 0); hidden(7, 1)
            hidden(7, 2); hidden(7, 3); hidden(7, 4); scale_down(6); hidden(7, 5); low_last(7); scale_down(7)

        @block.scalar
        def _(act):
            def col(c, rows=slice(0, P)):
                return tab[rows, c:c + 1]

            def quarter(h):
                return slice(h * TQ, (h + 1) * TQ)

            def weights(q):
                lo, hi = WGU_PARTS[q]
                act.wait_ge(wgu_in[q], 16)
                act.activation(wgu_r[:, :, lo:hi], wgu_int[:, :, lo:hi], ACT.Copy,
                               bias=-ZERO_POINT).then_inc(wgu_ready, 1)

            def last_down_weights():
                act.wait_ge(wd_in, 32)
                act.activation(wd_r[P - REM:P, FULL, :], wd_int[P - REM:P, FULL, :], ACT.Copy,
                               bias=-ZERO_POINT).then_inc(wd_last_ready, 1)

            def high_x(u):
                l = u if u < NQ else u + NQ
                b = full(act, ("xT", l))
                if u >= 2:
                    full(act, ("gate_up", u - 2, FC - 1))
                act.activation(xhi[:, u % 2, :, :], halves(b[:, :]), ACT.Copy).then_inc(xhi_ready, 1)

            def gate(u, j):
                n = FC * u + j
                if n == 0:
                    act.wait_ge(tab_in, 16)
                if n >= RING:
                    act.wait_ge(hf_ready, n - RING + 1)
                b = full(act, ("gate_up", u, j))
                rows, to = (P, 0) if j < FULL else (REM, P - REM)
                act.activation(silu[to:to + rows, n % RING, :], b[0:rows, 0:TQ], ACT.Silu,
                               scale=col(C_SG + j, slice(0, rows))).then_inc(silu_ready, 1)

            def high_h(u, j):
                n = FC * u + j
                act.wait_ge(hf_ready, n + 1)
                if u:
                    act.wait_ge(down_done, FC * (u - 1) + j + 1)
                rows = slice(0, P) if j < FULL else slice(P - REM, P)
                act.activation(hhi[rows, j, :], hf[rows, n % RING, :], ACT.Copy).then_inc(hhi_ready, 1)

            def attn_x(h):
                b = full(act, ("xT", NQ + h))
                act.activation(xlt[:, :, TQ * h + 1:TQ * (h + 1) + 1], halves(b[:, :]), ACT.Copy).then_inc(xlt_ready, 1)

            def low_rank_tanh(h):
                b = full(act, ("z", h))
                if h >= 2:
                    for m in MIXES:
                        full(act, ("rate", h - 2, m))
                act.activation(zt[:, h % 2, :], b[:, 0:TQ], ACT.Tanh).then_inc(z_ready, 1)
                act.activation(ztlast[:, h % 2, :], b[0:RLO, TQ:2 * TQ], ACT.Tanh).then_inc(z_ready, 1)

            def decay_tanh(h):
                b = full(act, ("w", h))
                if h >= 2:
                    full(act, ("w2", h - 2))
                act.activation(tw[:, h % 2, :], b[0:GLO, 0:TQ], ACT.Tanh).then_inc(tw_ready, 1)

            def decays(h):
                b = full(act, ("w2", h))
                if h:
                    act.wait_ge(decay_ready, h)
                act.activation(expw[:, :], b[:, 0:TQ], ACT.Exp, bias=col(C_BW)).then_inc(expw_ready, 1)
                act.wait_ge(expw_ready, h + 1)
                act.activation(decay[:, quarter(h)], expw[:, :], ACT.Exp, scale=-1.0).then_inc(decay_ready, 1)

            def values(h):
                b = full(act, ("v", h))
                if h >= 2:
                    act.wait_ge(bonus_v_ready, h - 1)
                    act.wait_ge(v_out[h - 2], 16)
                act.activation(vt[:, h % 2, :, :], halves(b[:, :]), ACT.Copy).then_inc(v_ready, 1)

            def keys(h):
                b = full(act, ("k", h))
                if h >= 2:
                    act.wait_ge(rbk_ready, h - 1)
                    act.wait_ge(scan_ready, HV * (h - 1))
                act.activation(kt[:, h % 2, :], b[:, 0:TQ], ACT.Copy).then_inc(k_ready, 1)

            def receptance(h):
                b = full(act, ("r", h))
                act.activation(rt[:, quarter(h)], b[:, 0:TQ], ACT.Copy).then_inc(r_ready, 1)

            def gates(h):
                b = full(act, ("g", h))
                act.activation(sg[:, h, :, :], halves(b[:, :]), ACT.Silu).then_inc(sg_ready, 1)

            def squares(h):
                act.wait_ge(oc_ready, h + 1)
                if h:
                    act.wait_ge(gvar_ready, h)
                act.activation(osq[:, :, :], oc[:, :, :], ACT.Square).then_inc(osq_ready, 1)

            def head_std(h):
                act.wait_ge(gvar_ready, h + 1)
                if h:
                    act.wait_ge(on_ready, h)
                act.activation(gstd[:, :, :], ssum[:, :, :], ACT.Sqrt).then_inc(gstd_ready, 1)

            def norm_affine(h):
                b = full(act, ("ofm", h))
                if h:
                    full(act, ("attn", h - 1))
                for c in range(KC):
                    act.activation(ogn[:, c, :], b[:, c * TQ:(c + 1) * TQ], ACT.Identity, scale=col(C_GNW + c),
                                   bias=col(C_GNB + c)).then_inc(ogn_ready, 1)

            weights(0); weights(1); weights(2); last_down_weights(); high_x(0); high_x(1); gate(0, 0); gate(0, 1)
            high_h(0, 0); high_h(0, 1); gate(0, 2); gate(0, 3); high_h(0, 2); gate(0, 4); high_h(0, 3); gate(0, 5)
            high_x(2); high_h(0, 4); high_h(0, 5); gate(1, 0); high_h(1, 0); gate(1, 1); gate(1, 2); high_h(1, 1)
            gate(1, 3); high_h(1, 2); gate(1, 4); high_h(1, 3); gate(1, 5); high_h(1, 4); attn_x(0); high_h(1, 5)
            gate(2, 0); high_x(3); gate(2, 1); high_h(2, 0); high_h(2, 1); low_rank_tanh(0); gate(2, 2); gate(2, 3)
            high_h(2, 2); high_h(2, 3); gate(2, 4); decay_tanh(0); values(0); gate(2, 5); gate(3, 0); keys(0)
            receptance(0); gates(0); high_h(2, 4); high_h(2, 5); high_h(3, 0); decays(0); attn_x(1); gate(3, 1)
            gate(3, 2); gate(3, 3); attn_x(2); high_h(3, 1); gate(3, 4); high_h(3, 2); low_rank_tanh(1)
            high_h(3, 3); high_h(3, 4); gate(3, 5); high_h(3, 5); decay_tanh(1); values(1); decays(1); attn_x(3)
            keys(1); receptance(1); squares(0); low_rank_tanh(2); gates(1); decay_tanh(2); head_std(0); values(2)
            norm_affine(0); decays(2); keys(2); low_rank_tanh(3); squares(1); receptance(2); head_std(1); gates(2)
            decay_tanh(3); values(3); keys(3); norm_affine(1); receptance(3); decays(3); high_x(4); squares(2)
            gates(3); gate(4, 0); gate(4, 1); high_h(4, 0); head_std(2); high_h(4, 1); gate(4, 2); gate(4, 3)
            high_x(5); high_h(4, 2); gate(4, 4); norm_affine(2); high_h(4, 3); high_h(4, 4); gate(4, 5); gate(5, 0)
            squares(3); high_h(4, 5); gate(5, 1); head_std(3); high_h(5, 0); gate(5, 2); norm_affine(3)
            high_h(5, 1); gate(5, 3); high_x(6); high_h(5, 2); gate(5, 4); high_h(5, 3); high_h(5, 4); gate(5, 5)
            gate(6, 0); high_h(5, 5); high_h(6, 0); gate(6, 1); gate(6, 2); high_h(6, 1); gate(6, 3); high_h(6, 2)
            gate(6, 4); high_h(6, 3); high_x(7); high_h(6, 4); gate(6, 5); high_h(6, 5); gate(7, 0); high_h(7, 0)
            gate(7, 1); high_h(7, 1); gate(7, 2); gate(7, 3); high_h(7, 2); high_h(7, 3); gate(7, 4); high_h(7, 4)
            gate(7, 5); high_h(7, 5)

        @block.gpsimd
        def _(pool):
            def constants():
                pool.memset(minus_half[:, :], -0.5).then_inc(consts, 1)
                pool.memset(xlt[:, :, 0:1], 0.0)
                pool.memset(state[:, :, 0:1], 0.0).then_inc(consts, 1)
                pool.wait_ge(consts, 2)

            def down_weights():
                pool.wait_ge(wd_in, 32)
                pool.tensor_scalar(wd_r[:, 0:FULL, :], wd_int[:, 0:FULL, :], -ZERO_POINT, None,
                                   ALU.add).then_inc(wd_ready, 1)
                pool.wait_ge(sdn_in, 16)
                pool.tensor_scalar(sdn[:, :], sdn[:, :], 0.5, None, ALU.mult).then_inc(consts, 1)

            def root(l):
                pool.wait_ge(var_ready, l + 1)
                pool.tensor_tensor(rstd[:, l, :], var_eps[:, l, :], minus_half[:, :], ALU.pow).then_inc(rstd_ready, 1)

            def low_h(u, j):
                pool.wait_ge(hhi_ready, FC * u + j + 1)
                if u:
                    pool.wait_ge(down_done, FC * (u - 1) + j + 1)
                pool.tensor_tensor(hlo[:, j, :], hf[:, (FC * u + j) % RING, :], hhi[:, j, :].bitcast(fp32),
                                   ALU.subtract).then_inc(hlo_ready, 1)

            def add_ffn(u):
                h = u % NQ
                pool.wait_ge(ffn_out_ready, u + 1)
                rows = xs[:, SUB * h:SUB * (h + 1), :]
                pool.tensor_tensor(rows, rows, ffn_out[:, u % 2, :, :], ALU.add).then_inc(residual_ready, 1)

            def add_x(h, m):
                n = mix_number(h, m)
                pool.wait_ge(scaled_ready, n + 1)
                pool.tensor_tensor(mix[:, n % MRING, :, :], mix[:, n % MRING, :, :],
                                   xlt[:, :, TQ * h + 1:TQ * (h + 1) + 1], ALU.add).then_inc(mix_ready, 1)

            def read_state(h, q):
                pool.wait_ge(scan_ready, HV * h + 2 * q + 2)
                pool.wait_ge(r_ready, h + 1)
                pool.tensor_tensor(vrep[:, h % 2, q, :, :],
                                   rt[:, h * TQ:(h + 1) * TQ].unsqueeze(1).to_broadcast([P, 2, TQ]),
                                   state[:, 2 * q:2 * q + 2, TQ * h:TQ * (h + 1)], ALU.mult).then_inc(read_ready[1], 1)

            constants(); root(0); down_weights(); root(1); root(2); root(3); low_h(0, 0); low_h(0, 1); low_h(0, 2)
            low_h(0, 3); low_h(0, 4); add_ffn(0); low_h(1, 0); low_h(1, 1); root(4); low_h(1, 2); low_h(1, 3)
            low_h(1, 4); low_h(2, 0); low_h(2, 1); low_h(2, 2); add_x(0, "w"); add_x(0, "v"); low_h(2, 3)
            add_x(0, "k"); add_x(0, "r"); add_x(0, "g"); low_h(2, 4); add_ffn(1); low_h(3, 0); root(5); add_ffn(2)
            root(6); low_h(3, 1); low_h(3, 2); low_h(3, 3); low_h(3, 4); read_state(0, 2); add_x(1, "w")
            add_x(1, "v"); read_state(0, 3); add_ffn(3); root(7); add_x(1, "k"); add_x(1, "r"); add_x(1, "g")
            read_state(1, 2); read_state(1, 3); add_x(2, "w"); add_x(2, "v"); add_x(2, "k"); add_x(2, "r")
            add_x(2, "g"); add_x(3, "w"); add_x(3, "v"); add_x(3, "k"); add_x(3, "r"); root(8); read_state(2, 2)
            read_state(2, 3); add_x(3, "g"); root(9); low_h(4, 0); low_h(4, 1); read_state(3, 2); read_state(3, 3)
            low_h(4, 2); low_h(4, 3); low_h(4, 4); root(10); low_h(5, 0); add_ffn(4); low_h(5, 1); low_h(5, 2)
            low_h(5, 3); low_h(5, 4); root(11); low_h(6, 0); low_h(6, 1); low_h(6, 2); low_h(6, 3); low_h(6, 4)
            add_ffn(5); low_h(7, 0); low_h(7, 1); low_h(7, 2); low_h(7, 3); low_h(7, 4); add_ffn(6); add_ffn(7)

        @block.sync
        def _(sp):
            def load(dst, src, ready):
                sp.dma_start(dst, src).then_inc(ready, 16)

            xv = x[0, :, :].rearrange("(n p) d -> p n d", p=P)
            wguv = wgu.rearrange("(c p) f -> p c f", p=P)

            def load_x(h):
                load(xs[:, SUB * h:SUB * (h + 1), :], xv[:, SUB * h:SUB * (h + 1), :], x_in[h])

            load_x(0)
            load(idt[:, :], ident, idt_in)
            load(rept[:, :], rep, idt_in)
            for q, (lo, hi) in enumerate(WGU_PARTS):
                load(wgu_int[:, :, lo:hi], wguv[:, :, lo:hi], wgu_in[q])
                if q == 0:
                    load(tab[:, :], table, tab_in)
                    load_x(1)
            load(wd_int[:, 0:FULL, :], wd[0:FULL * P, :].rearrange("(c p) d -> p c d", p=P), wd_in)
            load(wd_int[P - REM:P, FULL, :], wd[FULL * P:F, :], wd_in)
            load(sdn[:, :], sdown.partition_broadcast(P), sdn_in)
            load_x(2)
            load_x(3)
            load(wx1s[:, :, :], wx1.rearrange("(c p) f -> p c f", p=P), wz_in)
            load(wx2s[:, :], wx2[0:P, :], wz_in)
            load(wx2last[:, :], wx2[P:MIX * RLO, :], wz_in)
            for dst, src in ((ww1s, ww1), (wvs, wv), (wks, wk), (wrs, wr), (wgs, wg), (wos, wo)):
                load(dst[:, :, :], src.rearrange("(c p) f -> p c f", p=P), wp_in)
            load(ww2s[:, :], ww2, wp_in)
            for h in range(NQ):
                sp.wait_ge(v_ready, h + 1)
                sp.dma_start(v_dram[h, :, :], vt[:, h % 2, :, :].rearrange("p c t -> p (c t)")).then_inc(v_out[h], 16)
                sp.wait_ge(v_out[h], 16)
                if h >= 2:
                    sp.wait_ge(key_summed, PAIRS * (h - 1))
                for k in range(HQK):
                    sp.dma_start(vrep[k * NH:(k + 1) * NH, h % 2, :, :, :].rearrange("n q c t -> n q (c t)"),
                                 v_dram[h, :, :].rearrange("(q n) t -> n q t", n=NH)).then_inc(vrep_in[h], 16)
            outv = out[0, :, :].rearrange("(n p) d -> p n d", p=P)
            for h in range(NQ):
                sp.wait_ge(residual_ready, NQ + h + 1)
                s = SUB * h
                sp.dma_start(outv[:, s:s + SUB, :], xs[:, s:s + SUB, :]).then_inc(stored, 16)
            sp.wait_ge(stored, 16 * NQ)


def kernel(**inputs):
    import numpy as _np
    import concourse.bacc as _bacc
    from concourse import mybir as _mybir
    from concourse.bass_utils import run_bass_kernel_spmd as _run

    a = {n.replace("L0_attn_", "").replace("L0_ffn_", ""): _np.asarray(v) for n, v in inputs.items()}

    def by_key(w):
        return w.reshape(-1, NH, HQK).transpose(0, 2, 1).reshape(-1, NH * HQK)

    def by_value(w):
        return w.reshape(-1, NH, HV).transpose(0, 2, 1).reshape(-1, NH * HV)

    gate, up = a["wq_gate"].T, a["wq_up"].T
    parts = [w[:, j * P:(j + 1) * P] for j in range(FULL) for w in (gate, up)]
    parts += [gate[:, FULL * P:], up[:, FULL * P:]]

    table = _np.zeros((P, C_ALL), _np.float32)
    table[:, C_SG:C_SG + FULL] = a["s_gate"][:FULL * P].reshape(FULL, P).T
    table[:REM, C_SG + FULL] = a["s_gate"][FULL * P:]
    table[:, C_SU:C_SU + FULL] = a["s_up"][:FULL * P].reshape(FULL, P).T
    table[P - REM:, C_SU + FULL] = a["s_up"][FULL * P:]
    table[:, C_MU:C_MU + 2] = a["mu_x"].reshape(KC, P).T
    table[:, C_BW] = by_key(a["bw"])[0]
    table[:, C_BONUS] = by_key(a["bonus"].reshape(-1))[0]
    table[:, C_GNW:C_GNW + 2] = _np.repeat(a["gn_w"], NH).reshape(KC, P).T
    table[:, C_GNB:C_GNB + 2] = _np.repeat(a["gn_b"], NH).reshape(KC, P).T

    arrays = {
        "x": a["hidden_states"], "wgu": _np.concatenate(parts, 1), "wd": a["wq_down"].T, "table": table,
        "sdown": a["s_down"], "wx1": a["Wx1"], "wx2": a["Wx2"].reshape(MIX * RLO, D),
        "wr": by_key(a["Wr"]), "wk": by_key(a["Wk"]), "wv": by_value(a["Wv"]), "wg": by_value(a["Wg"]),
        "ww1": a["Ww1"], "ww2": by_key(a["Ww2"]),
        "wo": a["Wo"].reshape(NH, HV, D).transpose(1, 0, 2).reshape(NH * HV, D),
        "ident": _np.eye(P, dtype=_np.float32),
        "rep": _np.tile(_np.eye(NH, dtype=_np.float32), (4, 4)),
    }
    nc = _bacc.Bacc("TRN2", target_bir_lowering=False, num_devices=1)
    arrays = {n: _np.ascontiguousarray(v) for n, v in arrays.items()}
    args = [nc.dram_tensor(n, v.shape, _mybir.dt.from_np(v.dtype), kind="ExternalInput").ap()
            for n, v in arrays.items()]
    out = nc.dram_tensor("out", (1, T, D), _mybir.dt.float32, kind="ExternalOutput").ap()
    macaron(nc, *args, out)
    r = _run(nc, [arrays], core_ids=[0])
    return r.results[0]["out"]
```

```python
from contextlib import ExitStack

import concourse.bass as bass
import numpy as np
from concourse import mybir

T, D, F = 1024, 256, 704
P = 128
NQ = 4
TQ = T // NQ
SUB = TQ // P
KC = D // P
FULL = F // P
REM = F - FULL * P
FC = FULL + 1
WGU = (2 * FULL + 1) * P
NH, HQK, HV = 32, 4, 8
PAIRS = HV // 2
RLO, GLO, MIX = 32, 64, 5
ZROWS = 3 * RLO
QUADRANTS = P // RLO
WARM_UP = 3
EPS = 1e-5
ZERO_POINT = 128.0
OWN_SIGNAL = ("o", "down")
RING = 3
STACKS = (("w", "v"), ("k", "r"), ("g",))
MRING = 4

C_SG, C_SU, C_MU, C_BW, C_BONUS, C_GNW, C_GNB = 0, FC, 2 * FC, 2 * FC + 2, 2 * FC + 3, 2 * FC + 4, 2 * FC + 6
C_ALL = 2 * FC + 8

MIXES = ["w", "v", "k", "r", "g"]
INDEX = {"r": 0, "w": 1, "k": 2, "v": 3, "g": 4}
POOL_READS = ((0, 1), (0, 3), (1, 0), (1, 2), (1, 3), (2, 0), (2, 2), (2, 3), (3, 0), (3, 1), (3, 2), (3, 3))
WGU_PARTS = ((0, 256), (256, 768), (768, WGU))
WD_PARTS = ((0, 2), (2, FULL))


def macaron(nc, x, wgu, wd, table, sdown, wx1, wx2, wr, wk, wv, wg, ww1, ww2, wo, ident, rep, selector, out):
    fp32, fp32r, int32 = mybir.dt.float32, mybir.dt.float32r, mybir.dt.int32
    ALU, ACT, AX = mybir.AluOpType, mybir.ActivationFunctionType, mybir.AxisListType
    ctx = ExitStack()
    with ctx:
        def sb(name, shape, dt=fp32):
            return ctx.enter_context(nc.sbuf_tensor(name, shape, dt))

        def sem(name):
            return ctx.enter_context(nc.semaphore(name))

        xs = sb("xs", [P, T // P, D])
        tab = sb("tab", [P, C_ALL])
        sdn = sb("sdn", [P, D])
        idt = sb("idt", [P, P])
        rept = sb("rept", [P, P])
        minus_half = sb("minus_half", [P, SUB])
        unused = sb("unused", [P, SUB])
        wgu_int = sb("wgu_int", [P, KC, WGU], int32)
        wgu_r = sb("wgu_r", [P, KC, WGU], fp32r)
        wd_int = sb("wd_int", [P, FC, D], int32)
        wd_r = sb("wd_r", [P, FC, D], fp32r)
        wx1s = sb("wx1s", [P, KC, 2 * ZROWS])
        select_r = sb("select_r", [ZROWS, 6, P], fp32r)
        wx2_stack = sb("wx2_stack", [P, MIX, D], fp32r)
        wrs = sb("wrs", [P, KC, P])
        wks = sb("wks", [P, KC, P])
        wvs = sb("wvs", [P, KC, D])
        wgs = sb("wgs", [P, KC, D])
        ww1s = sb("ww1s", [P, KC, GLO])
        ww2s = sb("ww2s", [GLO, P])
        wos = sb("wos", [P, KC, D])

        stats = sb("stats", [P, 3 * NQ, SUB, 6])
        mv = sb("mv", [P, 3 * NQ, SUB, 2])
        var_eps = sb("var_eps", [P, 3 * NQ, SUB])
        rstd = sb("rstd", [P, 3 * NQ, SUB])
        minus_mean = sb("minus_mean", [P, 3 * NQ, SUB])
        norm_bias = sb("norm_bias", [P, 3 * NQ, SUB])
        xn = sb("xn", [P, 2, SUB, D])

        xhi = sb("xhi", [P, 2, KC, TQ], fp32r)
        xlo = sb("xlo", [P, 2, KC, TQ], fp32r)
        silu = sb("silu", [P, RING, TQ])
        hf = sb("hf", [P, RING, TQ])
        hhi = sb("hhi", [P, FC, TQ], fp32r)
        hlo = sb("hlo", [P, FC, TQ], fp32r)
        ffn_out = sb("ffn_out", [P, 2, SUB, D])

        xlt = sb("xlt", [P, KC, T + 1])
        delta = sb("delta", [P, 2, KC, TQ])
        xmu = sb("xmu", [P, 2, KC, TQ])
        z = sb("z", [ZROWS, 2, TQ])
        z_parts = sb("z_parts", [ZROWS, 2, 2, TQ], fp32r)
        z_stack = sb("z_stack", [P, 2, MIX, TQ], fp32r)
        reused = [w[:, :, :].rearrange("p c f -> p (c f)").bitcast(fp32) for w in (wgu_int, wd_int)]
        taken = [0, 0]

        def reuse(a, *shape):
            size = int(np.prod(shape))
            taken[a] += size
            names = " ".join("abc"[:len(shape)])
            return reused[a][:, taken[a] - size:taken[a]].rearrange(
                f"p ({names}) -> p {names}", **{n: v for n, v in zip("abc", shape)})

        mix = sb("mix", [P, MRING, KC, TQ])
        mix_flat = mix[:, :, :, :].rearrange("p n c t -> p (n c t)")
        wx2_raw = mix_flat[:, 0:MIX * D].rearrange("p (m d) -> p m d", m=MIX)
        select = mix_flat[0:ZROWS, MIX * D:MIX * D + 6 * P].rearrange("p (a q) -> p a q", a=6)
        tw = sb("tw", [GLO, 2, TQ])
        decay = sb("decay", [P, 2, TQ])
        vt = sb("vt", [P, 2, KC, TQ])
        kt = sb("kt", [P, 2, TQ])
        rt = sb("rt", [P, 2, TQ])
        sg = sb("sg", [P, NQ, KC, TQ])
        rbk = reuse(1, 2, TQ)
        bonus_v = reuse(1, 2, KC, TQ)
        vrep = sb("vrep", [P, 2, PAIRS, 2, TQ])
        state = sb("state", [P, HV, T + 1])
        ot = reuse(0, KC, TQ)
        vsum = sb("vsum", [P, SUB, NH])
        oc = reuse(0, SUB, D)
        ssum = sb("ssum", [P, SUB, NH])
        gstd = sb("gstd", [P, SUB, NH])
        ogn = reuse(0, KC, TQ)
        osq = ogn
        v_dram = nc.dram_tensor("v_dram", (NQ, P, KC * TQ), fp32, kind="Internal").ap()

        bank = [ctx.enter_context(nc.psum_tensor(f"bank{b}", [P, 2 * TQ], fp32)) for b in range(8)]
        bank_full = [sem(f"bank_full{b}") for b in range(8)]

        x_in = [sem(f"x_in{h}") for h in range(NQ)]
        wgu_in = [sem(f"wgu_in{q}") for q in range(len(WGU_PARTS))]
        wd_in = [sem(f"wd_in{q}") for q in range(len(WD_PARTS))]
        wd_last_in = sem("wd_last_in")
        tab_in = sem("tab_in")
        sdn_in = sem("sdn_in")
        idt_in = sem("idt_in")
        wz_in = sem("wz_in")
        wx2_in = sem("wx2_in")
        wx2_hi_ready = sem("wx2_hi_ready")
        wx2_ready = sem("wx2_ready")
        z_hi_ready = sem("z_hi_ready")
        z_lo_ready = sem("z_lo_ready")
        z_stack_ready = sem("z_stack_ready")
        select_ready = sem("select_ready")
        zeros_ready = sem("zeros_ready")
        wp_in = sem("wp_in")
        stored = sem("stored")
        v_out = [sem(f"v_out{h}") for h in range(NQ)]
        vrep_in = [sem(f"vrep_in{h}") for h in range(NQ)]
        wgu_ready = sem("wgu_ready")
        wd_ready = sem("wd_ready")
        wd_last_ready = sem("wd_last_ready")
        consts = sem("consts")
        dve_seq = sem("dve_seq")
        var_ready = sem("var_ready")
        mean_ready = sem("mean_ready")
        rstd_ready = sem("rstd_ready")
        norm_ready = sem("norm_ready")
        xn_ready = sem("xn_ready")
        xhi_ready = sem("xhi_ready")
        xlo_ready = sem("xlo_ready")
        silu_ready = sem("silu_ready")
        hf_ready = sem("hf_ready")
        hhi_ready = sem("hhi_ready")
        hlo_ready = sem("hlo_ready")
        hlo_last_ready = sem("hlo_last_ready")
        down_done = sem("down_done")
        ffn_out_ready = sem("ffn_out_ready")
        residual_ready = sem("residual_ready")
        attn_added = sem("attn_added")
        xlt_ready = sem("xlt_ready")
        xmu_ready = sem("xmu_ready")
        z_ready = sem("z_ready")
        scaled_ready = sem("scaled_ready")
        mix_ready = sem("mix_ready")
        tw_ready = sem("tw_ready")
        expw_ready = sem("expw_ready")
        decay_ready = sem("decay_ready")
        v_ready = sem("v_ready")
        k_ready = sem("k_ready")
        r_ready = sem("r_ready")
        sg_ready = sem("sg_ready")
        rbk_ready = sem("rbk_ready")
        bonus_v_ready = sem("bonus_v_ready")
        kv_ready = sem("kv_ready")
        scan_ready = sem("scan_ready")
        read_ready = [sem("read_ready_dve"), sem("read_ready_pool")]
        key_summed = sem("key_summed")
        ot_ready = sem("ot_ready")
        oc_ready = sem("oc_ready")
        osq_ready = sem("osq_ready")
        gvar_ready = sem("gvar_ready")
        gstd_ready = sem("gstd_ready")
        on_ready = sem("on_ready")
        ogn_ready = sem("ogn_ready")
        gated_ready = sem("gated_ready")

        def norm_use(l):
            return l if l < NQ else l - NQ if l >= 2 * NQ else None

        def mix_number(h, m):
            return MIX * h + MIXES.index(m)

        def read_out(name):
            kind, i = name[0], name[1]
            if kind == "xT":
                u = norm_use(i)
                return (xlt_ready, i - NQ + 1) if u is None else (xlo_ready, u + 1)
            if kind == "gate_up":
                return hf_ready, FC * i + name[2] + 1
            if kind == "stack":
                return z_stack_ready, len(STACKS) * i + name[2] + 1
            if kind == "rate":
                return scaled_ready, mix_number(i, name[2]) + 1
            ready, per = {"down": (ffn_out_ready, 1), "z": (z_ready, 1), "w": (tw_ready, 1), "v": (v_ready, 1),
                          "k": (k_ready, 1), "r": (r_ready, 1), "g": (sg_ready, 1), "w2": (expw_ready, 1),
                          "bonus": (bonus_v_ready, 1), "o": (ot_ready, 1), "otm": (oc_ready, 1),
                          "ofm": (ogn_ready, 2), "attn": (attn_added, 1)}[kind]
            return ready, per * (i + 1)

        fills = {}
        filled = [[] for _ in range(8)]

        def full(eng, name):
            b, n = fills[name]
            eng.wait_ge(bank_full[b], n + 1)
            return bank[b]

        def halves(tile):
            return tile.rearrange("p (a t) -> p a t", a=2)

        block = ctx.enter_context(nc.Block())

        @block.tensor
        def _(pe):
            def take(b, name):
                if filled[b]:
                    ready, value = read_out(filled[b][-1])
                    pe.wait_ge(ready, value)
                fills[name] = (b, sum(other[0] not in OWN_SIGNAL for other in filled[b]))
                filled[b].append(name)
                return bank[b]

            turns = {0: [0, 4], 4: [0, 2], 6: [0, 2]}

            def take_next(group, name):
                turn = turns[group]
                turn[0] += 1
                return take(group + (turn[0] - 1) % turn[1], name)

            def done(ins, name):
                ins.then_inc(bank_full[fills[name][0]], 1)

            def transpose_x(l):
                pe.wait_ge(xn_ready, l + 1)
                b = take_next(6, ("xT", l))
                for c in range(KC):
                    for s in range(SUB):
                        ins = pe.transpose(b[:, c * TQ + s * P:c * TQ + (s + 1) * P],
                                           xn[:, l % 2, s, c * P:(c + 1) * P], idt[:, :])
                done(ins, ("xT", l))

            def gate_up(u, j):
                if u == 0:
                    pe.wait_ge(wgu_ready, 1 + sum(2 * j * P >= lo for lo, _ in WGU_PARTS[1:]))
                b = take_next(0, ("gate_up", u, j))
                for a in range(2 if j < FULL else 1):
                    w = (2 * j + a) * P
                    for n, part in enumerate((xhi, xlo)):
                        if j == 0 and a == 0:
                            pe.wait_ge((xhi_ready, xlo_ready)[n], u + 1)
                        for c in range(KC):
                            ins = pe.matmul(b[:, a * TQ:(a + 1) * TQ], wgu_r[:, c, w:w + P], part[:, u % 2, c, :],
                                            start=(n == 0 and c == 0), stop=(n == 1 and c == KC - 1))
                done(ins, ("gate_up", u, j))

            def down(u, j):
                if u == 0 and j < FULL:
                    pe.wait_ge(wd_ready, 1 + (j >= WD_PARTS[1][0]))
                if j == 0:
                    take_next(4, ("down", u))
                b = bank[fills["down", u][0]]
                lo = 0 if j < FULL else P - REM
                if u == 0 and j == FULL:
                    pe.wait_ge(wd_last_ready, 1)
                for n, part in enumerate((hhi, hlo)):
                    if n == 0:
                        pe.wait_ge(hhi_ready, FC * u + j + 1)
                    elif j < FULL:
                        pe.wait_ge(hlo_ready, FULL * u + j + 1)
                    else:
                        pe.wait_ge(hlo_last_ready, u + 1)
                    for s in range(SUB):
                        ins = pe.matmul(b[:, s * D:(s + 1) * D], part[lo:P, j, s * P:(s + 1) * P], wd_r[lo:P, j, :],
                                        start=(j == 0 and n == 0 and s == 0), stop=(j == FC - 1 and n == 1),
                                        skip_group_check=True)
                ins.then_inc(down_done, 1)

            def low_rank(h):
                if h == 0:
                    pe.wait_ge(wz_in, 32)
                pe.wait_ge(xmu_ready, KC * (h + 1))
                b = take_next(0, ("z", h))
                for a in range(2):
                    for c in range(KC):
                        ins = pe.matmul(b[0:ZROWS, a * TQ:(a + 1) * TQ], wx1s[:, c, a * ZROWS:(a + 1) * ZROWS],
                                        xmu[:, h % 2, c, :], start=(c == 0), stop=(c == KC - 1))
                done(ins, ("z", h))

            def stack(h, g):
                if h == 0 and g == 0:
                    pe.wait_ge(select_ready, 1)
                b = take_next(0, ("stack", h, g))
                for n, m in enumerate(STACKS[g]):
                    a, at = divmod(INDEX[m] * RLO, ZROWS)
                    for part, ready in enumerate((z_hi_ready, z_lo_ready)):
                        if g == 0 and n == 0:
                            pe.wait_ge(ready, h + 1)
                        ins = pe.matmul(b[:, n * TQ:(n + 1) * TQ], select_r[:, 2 * (at // RLO) + part, :], z_parts[:, part, a, :],
                                        start=(part == 0), stop=(part == 1))
                done(ins, ("stack", h, g))

            def mix_rate(h, m):
                if h == 0 and m == MIXES[0]:
                    pe.wait_ge(wx2_ready, 1)
                g = [m in group for group in STACKS].index(True)
                pe.wait_ge(z_stack_ready, len(STACKS) * h + g + 1)
                b = take_next(0, ("rate", h, m))
                for c in range(KC):
                    ins = pe.matmul(b[:, c * TQ:(c + 1) * TQ], wx2_stack[:, INDEX[m], c * P:(c + 1) * P],
                                    z_stack[:, h % 2, MIXES.index(m), :], start=True, stop=True)
                done(ins, ("rate", h, m))

            def project(h, m):
                w, outs = {"w": (ww1s, (GLO,)), "v": (wvs, (P, P)), "k": (wks, (P,)),
                           "r": (wrs, (P,)), "g": (wgs, (P, P))}[m]
                n = mix_number(h, m)
                if n == 0:
                    pe.wait_ge(wp_in, 128)
                pe.wait_ge(mix_ready, n + 1)
                b = take_next(0, (m, h))
                for o, rows in enumerate(outs):
                    for c in range(KC):
                        ins = pe.matmul(b[0:rows, o * TQ:(o + 1) * TQ], w[:, c, o * P:o * P + rows],
                                        mix[:, n % MRING, c, :], start=(c == 0), stop=(c == KC - 1))
                done(ins, (m, h))

            def decay_logit(h):
                pe.wait_ge(tw_ready, h + 1)
                b = take_next(0, ("w2", h))
                done(pe.matmul(b[:, 0:TQ], ww2s[:, :], tw[:, h % 2, :], start=True, stop=True), ("w2", h))

            def bonus_sum(h):
                pe.wait_ge(rbk_ready, h + 1)
                b = take_next(0, ("bonus", h))
                done(pe.matmul(b[:, 0:TQ], rept[:, :], rbk[:, h % 2, :], start=True, stop=True), ("bonus", h))

            def key_sum(h, q):
                if q == 0:
                    take_next(6, ("o", h))
                b = bank[fills["o", h][0]]
                reader = (h, q) in POOL_READS
                pe.wait_ge(read_ready[reader], sum(((a, b) in POOL_READS) == reader
                                                   for a in range(h + 1) for b in range(PAIRS) if (a, b) <= (h, q)))
                pe.matmul(b[q * NH:(q + 1) * NH, :], rept[:, 0:NH], vrep[:, h % 2, q, :, :],
                          start=True, stop=True).then_inc(key_summed, 1)

            def o_token_major(h):
                pe.wait_ge(ot_ready, h + 1)
                b = take_next(6, ("otm", h))
                for s in range(SUB):
                    for c in range(KC):
                        ins = pe.transpose(b[:, s * D + c * P:s * D + (c + 1) * P], ot[:, c, s * P:(s + 1) * P],
                                           idt[:, :])
                done(ins, ("otm", h))

            def o_feature_major(h):
                pe.wait_ge(on_ready, h + 1)
                b = take_next(6, ("ofm", h))
                for c in range(KC):
                    for s in range(SUB):
                        ins = pe.transpose(b[:, c * TQ + s * P:c * TQ + (s + 1) * P], oc[:, s, c * P:(c + 1) * P],
                                           idt[:, :])
                done(ins, ("ofm", h))

            def output(h):
                pe.wait_ge(gated_ready, h + 1)
                b = take_next(6, ("attn", h))
                for s in range(SUB):
                    for c in range(KC):
                        ins = pe.matmul(b[:, s * D:(s + 1) * D], ogn[:, c, s * P:(s + 1) * P], wos[:, c, :],
                                        start=(c == 0), stop=(c == KC - 1))
                done(ins, ("attn", h))

            pe.wait_ge(zeros_ready, 1)
            for _ in range(WARM_UP):
                pe.matmul(bank[5][:, :], vrep[:, 1, 0, 0, 0:P], vrep[:, 1, 0, :, :], start=True, stop=True)
            pe.wait_ge(idt_in, 16)
            transpose_x(0); gate_up(0, 0); transpose_x(1); gate_up(0, 1); gate_up(0, 2); gate_up(0, 3)
            gate_up(0, 4); down(0, 0); gate_up(0, 5); down(0, 1); gate_up(1, 0); down(0, 2); transpose_x(2)
            gate_up(1, 1); down(0, 3); gate_up(1, 2); down(0, 4); gate_up(1, 3); down(0, 5); gate_up(1, 4)
            down(1, 0); gate_up(1, 5); down(1, 1); gate_up(2, 0); transpose_x(3); gate_up(2, 1); down(1, 2)
            gate_up(2, 2); down(1, 3); transpose_x(4); down(1, 4); gate_up(2, 3); down(1, 5); gate_up(2, 4)
            low_rank(0); down(2, 0); gate_up(2, 5); down(2, 1); gate_up(3, 0); down(2, 2); down(2, 3); stack(0, 0)
            gate_up(3, 1); mix_rate(0, "w"); down(2, 4); mix_rate(0, "v"); stack(0, 1); transpose_x(5); down(2, 5)
            stack(0, 2); mix_rate(0, "k"); project(0, "w"); mix_rate(0, "r"); project(0, "v"); low_rank(1)
            gate_up(3, 2); mix_rate(0, "g"); decay_logit(0); down(3, 0); project(0, "k"); down(3, 1); stack(1, 0)
            project(0, "r"); mix_rate(1, "w"); stack(1, 1); mix_rate(1, "v"); gate_up(3, 3); project(0, "g")
            transpose_x(6); project(1, "w"); stack(1, 2); project(1, "v"); gate_up(3, 4); low_rank(2); key_sum(0, 0)
            mix_rate(1, "k"); gate_up(3, 5); mix_rate(1, "r"); key_sum(0, 1); bonus_sum(0); key_sum(0, 2)
            mix_rate(1, "g"); stack(2, 0); key_sum(0, 3); mix_rate(2, "w"); project(1, "k"); mix_rate(2, "v")
            o_token_major(0); project(1, "r"); stack(2, 1); down(3, 2); decay_logit(1); down(3, 3); mix_rate(2, "k")
            down(3, 4); stack(2, 2); down(3, 5); project(1, "g"); project(2, "w"); project(2, "v"); bonus_sum(1)
            decay_logit(2); o_feature_major(0); project(2, "k"); transpose_x(7); key_sum(1, 0); mix_rate(2, "r")
            key_sum(1, 1); output(0); low_rank(3); key_sum(1, 2); mix_rate(2, "g"); key_sum(1, 3); project(2, "r")
            stack(3, 0); stack(3, 1); mix_rate(3, "w"); o_token_major(1); mix_rate(3, "v"); transpose_x(8)
            project(2, "g"); project(3, "w"); gate_up(4, 0); bonus_sum(2); project(3, "v"); mix_rate(3, "k")
            mix_rate(3, "r"); gate_up(4, 1); o_feature_major(1); key_sum(2, 0); gate_up(4, 2); decay_logit(3)
            output(1); project(3, "k"); key_sum(2, 1); gate_up(4, 3); key_sum(2, 2); key_sum(2, 3); project(3, "r")
            stack(3, 2); o_token_major(2); transpose_x(9); down(4, 0); gate_up(4, 4); down(4, 1); down(4, 2)
            gate_up(4, 5); key_sum(3, 0); key_sum(3, 1); bonus_sum(3); key_sum(3, 2); gate_up(5, 0); key_sum(3, 3)
            o_feature_major(2); mix_rate(3, "g"); down(4, 3); gate_up(5, 1); o_token_major(3); output(2); down(4, 4)
            gate_up(5, 2); project(3, "g"); gate_up(5, 3); gate_up(5, 4); down(4, 5); o_feature_major(3); down(5, 0)
            down(5, 1); transpose_x(10); gate_up(5, 5); output(3); gate_up(6, 0); down(5, 2); gate_up(6, 1)
            down(5, 3); gate_up(6, 2); down(5, 4); gate_up(6, 3); down(5, 5); transpose_x(11); gate_up(6, 4)
            down(6, 0); gate_up(6, 5); down(6, 1); gate_up(7, 0); down(6, 2); gate_up(7, 1); down(6, 3)
            gate_up(7, 2); down(6, 4); gate_up(7, 3); down(6, 5); gate_up(7, 4); down(7, 0); gate_up(7, 5)
            down(7, 1); down(7, 2); down(7, 3); down(7, 4); down(7, 5)

        @block.vector
        def _(dve):
            steps = [0]

            def step(ins):
                steps[0] += 1
                ins.then_inc(dve_seq, 1)

            def settle():
                dve.wait_ge(dve_seq, steps[0])

            def col(c, rows=slice(0, P)):
                return tab[rows, c:c + 1]

            def quarter(h):
                return slice(h * TQ, (h + 1) * TQ)

            def rows_of(h):
                return xs[:, SUB * h:SUB * (h + 1), :]

            def down_weights(q):
                lo, hi = WD_PARTS[q]
                dve.wait_ge(wd_in[q], 16)
                dve.tensor_scalar(wd_r[:, lo:hi, :], wd_int[:, lo:hi, :], -ZERO_POINT, None,
                                  ALU.add).then_inc(wd_ready, 1)

            def low_wx2():
                dve.wait_ge(wx2_hi_ready, 1)
                rows = slice(P // 2, P)
                dve.tensor_tensor(wx2_stack[rows, :, :], wx2_raw[rows], wx2_stack[rows, :, :].bitcast(fp32),
                                  ALU.subtract).then_inc(wx2_ready, 1)

            def norm_stats(l):
                h = l % NQ
                if l < NQ:
                    dve.wait_ge(x_in[h], 16)
                elif l < 2 * NQ:
                    dve.wait_ge(residual_ready, h + 1)
                else:
                    dve.wait_ge(attn_added, h + 1)
                for s in range(SUB):
                    step(dve.bn_stats(stats[:, l, s, :], xs[:, SUB * h + s, :]))
                settle()
                for s in range(SUB):
                    step(dve.bn_aggr(mv[:, l, s, :], stats[:, l, s, :]))
                settle()
                dve.tensor_scalar(var_eps[:, l, :], mv[:, l, :, 1], EPS, None, ALU.add).then_inc(var_ready, 1)
                dve.tensor_scalar(minus_mean[:, l, :], mv[:, l, :, 0], -1.0, None, ALU.mult).then_inc(mean_ready, 1)

            def split_x(u):
                l = u if u < NQ else u + NQ
                dve.wait_ge(xhi_ready, u + 1)
                if u >= 2:
                    full(dve, ("gate_up", u - 2, FC - 1))
                b = full(dve, ("xT", l))
                dve.tensor_tensor(xlo[:, u % 2, :, :], halves(b[:, :]), xhi[:, u % 2, :, :].bitcast(fp32),
                                  ALU.subtract).then_inc(xlo_ready, 1)

            def hidden(u, j):
                n = FC * u + j
                if n == 0:
                    dve.wait_ge(tab_in, 16)
                dve.wait_ge(silu_ready, n + 1)
                if n >= RING:
                    v, i = divmod(n - RING, FC)
                    dve.wait_ge(hhi_ready, n - RING + 1)
                    if i < FULL:
                        dve.wait_ge(hlo_ready, FULL * v + i + 1)
                    else:
                        dve.wait_ge(hlo_last_ready, v + 1)
                b = full(dve, ("gate_up", u, j))
                rows, at = (slice(0, P), TQ) if j < FULL else (slice(P - REM, P), 0)
                dve.scalar_tensor_tensor(hf[rows, n % RING, :], b[rows, at:at + TQ], col(C_SU + j, rows),
                                         silu[rows, n % RING, :], ALU.mult, ALU.mult).then_inc(hf_ready, 1)

            def low_last(u):
                n = FC * u + FULL
                dve.wait_ge(hhi_ready, n + 1)
                if u:
                    dve.wait_ge(down_done, FC * u)
                rows = slice(P - REM, P)
                dve.tensor_tensor(hlo[rows, FULL, :], hf[rows, n % RING, :], hhi[rows, FULL, :].bitcast(fp32),
                                  ALU.subtract).then_inc(hlo_last_ready, 1)

            def scale_down(u):
                dve.wait_ge(down_done, FC * (u + 1))
                if u == 0:
                    dve.wait_ge(consts, 3)
                if u >= 2:
                    dve.wait_ge(residual_ready, u - 1)
                b = bank[fills["down", u][0]]
                dve.tensor_tensor(ffn_out[:, u % 2, :, :], halves(b[:, :]),
                                  sdn[:, :].unsqueeze(1).to_broadcast([P, SUB, D]), ALU.mult).then_inc(ffn_out_ready, 1)

            def shift(h):
                if h == 0:
                    dve.wait_ge(consts, 2)
                dve.wait_ge(xlt_ready, h + 1)
                if h >= 2:
                    dve.wait_ge(scaled_ready, MIX * (h - 1))
                at = TQ * h
                step(dve.tensor_tensor(delta[:, h % 2, :, :], xlt[:, :, at:at + TQ], xlt[:, :, at + 1:at + TQ + 1],
                                       ALU.subtract))
                settle()
                if h >= 2:
                    full(dve, ("z", h - 2))
                for c in range(KC):
                    dve.scalar_tensor_tensor(xmu[:, h % 2, c, :], delta[:, h % 2, c, :], col(C_MU + c),
                                             xlt[:, c, at + 1:at + TQ + 1], ALU.mult, ALU.add).then_inc(xmu_ready, 1)

            def scale_delta(h, m):
                n = mix_number(h, m)
                if n >= MRING:
                    full(dve, (MIXES[(n - MRING) % MIX], (n - MRING) // MIX))
                if n == 0:
                    dve.wait_ge(wx2_ready, 1)
                if n == 2:
                    dve.wait_ge(select_ready, 1)
                b = full(dve, ("rate", h, m))
                dve.tensor_tensor(mix[:, n % MRING, :, :], halves(b[:, :]), delta[:, h % 2, :, :],
                                  ALU.mult).then_inc(scaled_ready, 1)

            def bonus_in(h):
                dve.wait_ge(r_ready, h + 1)
                dve.wait_ge(k_ready, h + 1)
                if h >= 2:
                    full(dve, ("bonus", h - 2))
                dve.scalar_tensor_tensor(rbk[:, h % 2, :], rt[:, h % 2, :], col(C_BONUS), kt[:, h % 2, :],
                                         ALU.mult, ALU.mult).then_inc(rbk_ready, 1)

            def bonus_out(h):
                b = full(dve, ("bonus", h))
                dve.wait_ge(v_ready, h + 1)
                dve.tensor_tensor(bonus_v[:, h % 2, :, :], b[:, 0:TQ].unsqueeze(1).to_broadcast([P, KC, TQ]),
                                  vt[:, h % 2, :, :], ALU.mult).then_inc(bonus_v_ready, 1)

            def key_value(h, q):
                dve.wait_ge(vrep_in[h], 16 * HQK)
                dve.wait_ge(k_ready, h + 1)
                kv = vrep[:, h % 2, q, :, :]
                dve.tensor_tensor(kv, kt[:, h % 2, :].unsqueeze(1).to_broadcast([P, 2, TQ]), kv,
                                  ALU.mult).then_inc(kv_ready, 1)

            def scans(h, q):
                dve.wait_ge(kv_ready, PAIRS * h + q + 1)
                dve.wait_ge(decay_ready, h + 1)
                at = TQ * h
                if h:
                    dve.wait_ge(scan_ready, HV * (h - 1) + 2 * q + 2)
                for a in range(2):
                    p = 2 * q + a
                    dve.tensor_tensor_scan(state[:, p, at + 1:at + TQ + 1], decay[:, h % 2, :],
                                           vrep[:, h % 2, q, a, :], state[:, p, at:at + 1],
                                           ALU.mult, ALU.add).then_inc(scan_ready, 1)

            def read_state(h, q):
                dve.wait_ge(scan_ready, HV * h + 2 * q + 2)
                dve.wait_ge(r_ready, h + 1)
                dve.tensor_tensor(vrep[:, h % 2, q, :, :], rt[:, h % 2, :].unsqueeze(1).to_broadcast([P, 2, TQ]),
                                  state[:, 2 * q:2 * q + 2, TQ * h:TQ * (h + 1)], ALU.mult).then_inc(read_ready[0], 1)

            def add_bonus(h):
                dve.wait_ge(key_summed, PAIRS * (h + 1))
                dve.wait_ge(bonus_v_ready, h + 1)
                if h:
                    full(dve, ("otm", h - 1))
                b = bank[fills["o", h][0]]
                dve.tensor_tensor(ot[:, :, :], halves(b[:, :]), bonus_v[:, h % 2, :, :], ALU.add).then_inc(ot_ready, 1)

            def by_head(tile):
                return tile.rearrange("p s (v n) -> p s v n", n=NH)

            def per_head(tile):
                return tile.unsqueeze(2).to_broadcast([P, SUB, HV, NH])

            def centre(h):
                b = full(dve, ("otm", h))
                step(dve.tensor_reduce(vsum[:, :, :], b[:, :].rearrange("p (s v n) -> p s n v", s=SUB, n=NH),
                                       AX.X, ALU.add))
                settle()
                if h:
                    full(dve, ("ofm", h - 1))
                for s in range(SUB):
                    ins = dve.scalar_tensor_tensor(by_head(oc[:, :, :])[:, s], per_head(vsum[:, :, :])[:, s], -1.0 / HV,
                                                   by_head(halves(b[:, :]))[:, s], ALU.mult, ALU.add)
                ins.then_inc(oc_ready, 1)

            def head_var(h):
                dve.wait_ge(osq_ready, h + 1)
                step(dve.tensor_reduce(ssum[:, :, :], osq[:, :, :].rearrange("p s (v n) -> p s n v", n=NH),
                                       AX.X, ALU.add))
                settle()
                dve.tensor_scalar(ssum[:, :, :], ssum[:, :, :], 1.0 / HV, EPS, ALU.mult, ALU.add).then_inc(gvar_ready, 1)

            def head_scale(h):
                dve.wait_ge(gstd_ready, h + 1)
                step(dve.reciprocal(gstd[:, :, :], gstd[:, :, :]))
                settle()
                dve.tensor_tensor(by_head(oc[:, :, :]), by_head(oc[:, :, :]), per_head(gstd[:, :, :]),
                                  ALU.mult).then_inc(on_ready, 1)

            def gate_o(h):
                dve.wait_ge(ogn_ready, KC * (h + 1))
                dve.wait_ge(sg_ready, h + 1)
                dve.tensor_tensor(ogn[:, :, :], ogn[:, :, :], sg[:, h, :, :], ALU.mult).then_inc(gated_ready, 1)

            def add_attn(h):
                b = full(dve, ("attn", h))
                dve.tensor_tensor(rows_of(h), halves(b[:, :]), rows_of(h), ALU.add).then_inc(attn_added, 1)

            norm_stats(0); norm_stats(1); split_x(0); norm_stats(2); hidden(0, 0); hidden(0, 1); down_weights(0)
            hidden(0, 2); split_x(1); hidden(0, 3); down_weights(1); hidden(0, 4); norm_stats(3); hidden(0, 5)
            hidden(1, 0); split_x(2); hidden(1, 1); low_last(0); scale_down(0); hidden(1, 2); hidden(1, 3)
            norm_stats(4); hidden(1, 4); hidden(1, 5); split_x(3); hidden(2, 0); hidden(2, 1); low_last(1)
            hidden(2, 2); shift(0); scale_down(1); hidden(2, 3); low_wx2(); hidden(2, 4); norm_stats(5)
            hidden(2, 5); low_last(2); hidden(3, 0); scale_delta(0, "w"); scale_delta(0, "v"); hidden(3, 1)
            scale_down(2); scale_delta(0, "k"); shift(1); scale_delta(0, "r"); norm_stats(6); hidden(3, 2)
            scale_delta(0, "g"); scale_delta(1, "w"); scale_delta(1, "v"); key_value(0, 0); key_value(0, 1)
            scans(0, 0); hidden(3, 3); key_value(0, 2); shift(2); read_state(0, 0); scans(0, 1); scans(0, 2)
            hidden(3, 4); bonus_in(0); key_value(0, 3); read_state(0, 2); scans(0, 3); hidden(3, 5)
            scale_delta(1, "k"); bonus_out(0); scale_delta(1, "r"); low_last(3); scale_delta(1, "g"); add_bonus(0)
            scale_delta(2, "w"); scale_delta(2, "v"); key_value(1, 0); centre(0); key_value(1, 1); bonus_in(1)
            head_var(0); scale_down(3); scale_delta(2, "k"); scans(1, 0); key_value(1, 2); norm_stats(7)
            head_scale(0); scans(1, 1); key_value(1, 3); read_state(1, 1); scans(1, 2); gate_o(0); bonus_out(1)
            shift(3); scans(1, 3); scale_delta(2, "r"); add_attn(0); norm_stats(8); key_value(2, 0)
            scale_delta(2, "g"); key_value(2, 1); add_bonus(1); scans(2, 0); scale_delta(3, "w"); centre(1)
            scale_delta(3, "v"); split_x(4); bonus_in(2); key_value(2, 2); head_var(1); scans(2, 1); hidden(4, 0)
            bonus_out(2); head_scale(1); scans(2, 2); key_value(2, 3); scale_delta(3, "k"); gate_o(1)
            scale_delta(3, "r"); scans(2, 3); read_state(2, 1); add_attn(1); hidden(4, 1); norm_stats(9)
            key_value(3, 0); hidden(4, 2); scans(3, 0); key_value(3, 1); add_bonus(2); scans(3, 1); hidden(4, 3)
            key_value(3, 2); centre(2); key_value(3, 3); scans(3, 2); head_var(2); bonus_in(3); scans(3, 3)
            split_x(5); head_scale(2); hidden(4, 4); bonus_out(3); hidden(4, 5); add_bonus(3); gate_o(2)
            scale_delta(3, "g"); centre(3); hidden(5, 0); hidden(5, 1); head_var(3); add_attn(2); low_last(4)
            norm_stats(10); head_scale(3); scale_down(4); hidden(5, 2); gate_o(3); hidden(5, 3); split_x(6)
            hidden(5, 4); add_attn(3); hidden(5, 5); norm_stats(11); hidden(6, 0); hidden(6, 1); low_last(5)
            hidden(6, 2); hidden(6, 3); split_x(7); scale_down(5); hidden(6, 4); hidden(6, 5); low_last(6)
            hidden(7, 0); hidden(7, 1); hidden(7, 2); scale_down(6); hidden(7, 3); hidden(7, 4); hidden(7, 5)
            low_last(7); scale_down(7)

        @block.scalar
        def _(act):
            def col(c, rows=slice(0, P)):
                return tab[rows, c:c + 1]

            def quarter(h):
                return slice(h * TQ, (h + 1) * TQ)

            def load_silu():
                act.wait_ge(consts, 1)
                act.activation(unused[:, :], minus_half[:, :], ACT.Silu)

            def weights(q):
                lo, hi = WGU_PARTS[q]
                act.wait_ge(wgu_in[q], 16)
                act.activation(wgu_r[:, :, lo:hi], wgu_int[:, :, lo:hi], ACT.Copy,
                               bias=-ZERO_POINT).then_inc(wgu_ready, 1)

            def last_down_weights():
                act.wait_ge(wd_last_in, 16)
                act.activation(wd_r[P - REM:P, FULL, :], wd_int[P - REM:P, FULL, :], ACT.Copy,
                               bias=-ZERO_POINT).then_inc(wd_last_ready, 1)

            def normalise(l):
                act.wait_ge(norm_ready, l + 1)
                if l >= 2:
                    full(act, ("xT", l - 2))
                for s in range(SUB):
                    ins = act.activation(xn[:, l % 2, s, :], xs[:, SUB * (l % NQ) + s, :], ACT.Identity,
                                         scale=rstd[:, l, s:s + 1], bias=norm_bias[:, l, s:s + 1])
                ins.then_inc(xn_ready, 1)

            def high_x(u):
                l = u if u < NQ else u + NQ
                b = full(act, ("xT", l))
                if u >= 2:
                    full(act, ("gate_up", u - 2, FC - 1))
                act.activation(xhi[:, u % 2, :, :], halves(b[:, :]), ACT.Copy).then_inc(xhi_ready, 1)

            def gate(u, j):
                n = FC * u + j
                if n == 0:
                    act.wait_ge(tab_in, 16)
                if n >= RING:
                    act.wait_ge(hf_ready, n - RING + 1)
                b = full(act, ("gate_up", u, j))
                rows, to = (P, 0) if j < FULL else (REM, P - REM)
                act.activation(silu[to:to + rows, n % RING, :], b[0:rows, 0:TQ], ACT.Silu,
                               scale=col(C_SG + j, slice(0, rows))).then_inc(silu_ready, 1)

            def high_h(u, j):
                n = FC * u + j
                act.wait_ge(hf_ready, n + 1)
                if u:
                    act.wait_ge(down_done, FC * (u - 1) + j + 1)
                rows = slice(0, P) if j < FULL else slice(P - REM, P)
                act.activation(hhi[rows, j, :], hf[rows, n % RING, :], ACT.Copy).then_inc(hhi_ready, 1)

            def attn_x(h):
                b = full(act, ("xT", NQ + h))
                act.activation(xlt[:, :, TQ * h + 1:TQ * (h + 1) + 1], halves(b[:, :]), ACT.Copy).then_inc(xlt_ready, 1)

            def low_rank_tanh(h):
                b = full(act, ("z", h))
                if h:
                    act.wait_ge(z_lo_ready, h)
                act.activation(z[:, :, :], halves(b[0:ZROWS, :]), ACT.Tanh).then_inc(z_ready, 1)

            def high_z(h):
                act.wait_ge(z_ready, h + 1)
                if h:
                    full(act, ("stack", h - 1, len(STACKS) - 1))
                act.activation(z_parts[:, 0, :, :], z[:, :, :], ACT.Copy).then_inc(z_hi_ready, 1)

            def stack_copy(h, g):
                b = full(act, ("stack", h, g))
                lo = MIXES.index(STACKS[g][0])
                if h >= 2:
                    for m in STACKS[g]:
                        full(act, ("rate", h - 2, m))
                size = len(STACKS[g])
                act.activation(z_stack[:, h % 2, lo:lo + size, :], halves(b[:, :])[:, 0:size, :],
                               ACT.Copy).then_inc(z_stack_ready, 1)

            def copy_select():
                act.wait_ge(wz_in, 32)
                act.activation(select_r[:, :, :], select, ACT.Copy).then_inc(select_ready, 1)

            def high_wx2():
                act.wait_ge(wx2_in, 16 * QUADRANTS)
                act.activation(wx2_stack[:, :, :], wx2_raw, ACT.Copy).then_inc(wx2_hi_ready, 1)

            def decay_tanh(h):
                b = full(act, ("w", h))
                if h >= 2:
                    full(act, ("w2", h - 2))
                act.activation(tw[:, h % 2, :], b[0:GLO, 0:TQ], ACT.Tanh).then_inc(tw_ready, 1)

            def decays(h):
                b = full(act, ("w2", h))
                if h >= 2:
                    act.wait_ge(scan_ready, HV * (h - 1))
                act.activation(decay[:, h % 2, :], b[:, 0:TQ], ACT.Exp, bias=col(C_BW)).then_inc(expw_ready, 1)
                act.wait_ge(expw_ready, h + 1)
                act.activation(decay[:, h % 2, :], decay[:, h % 2, :], ACT.Exp, scale=-1.0).then_inc(decay_ready, 1)

            def values(h):
                b = full(act, ("v", h))
                if h >= 2:
                    act.wait_ge(bonus_v_ready, h - 1)
                    act.wait_ge(v_out[h - 2], 16)
                act.activation(vt[:, h % 2, :, :], halves(b[:, :]), ACT.Copy).then_inc(v_ready, 1)

            def keys(h):
                b = full(act, ("k", h))
                if h >= 2:
                    act.wait_ge(rbk_ready, h - 1)
                    act.wait_ge(scan_ready, HV * (h - 1))
                act.activation(kt[:, h % 2, :], b[:, 0:TQ], ACT.Copy).then_inc(k_ready, 1)

            def receptance(h):
                b = full(act, ("r", h))
                if h >= 2:
                    act.wait_ge(rbk_ready, h - 1)
                    act.wait_ge(key_summed, PAIRS * (h - 1))
                act.activation(rt[:, h % 2, :], b[:, 0:TQ], ACT.Copy).then_inc(r_ready, 1)

            def gates(h):
                b = full(act, ("g", h))
                act.activation(sg[:, h, :, :], halves(b[:, :]), ACT.Silu).then_inc(sg_ready, 1)

            def squares(h):
                act.wait_ge(oc_ready, h + 1)
                if h:
                    full(act, ("attn", h - 1))
                act.activation(osq[:, :, :], oc[:, :, :], ACT.Square).then_inc(osq_ready, 1)

            def head_std(h):
                act.wait_ge(gvar_ready, h + 1)
                if h:
                    act.wait_ge(on_ready, h)
                act.activation(gstd[:, :, :], ssum[:, :, :], ACT.Sqrt).then_inc(gstd_ready, 1)

            def norm_affine(h):
                b = full(act, ("ofm", h))
                for c in range(KC):
                    act.activation(ogn[:, c, :], b[:, c * TQ:(c + 1) * TQ], ACT.Identity, scale=col(C_GNW + c),
                                   bias=col(C_GNB + c)).then_inc(ogn_ready, 1)

            load_silu(); weights(0); normalise(0); weights(1); high_x(0); normalise(1); weights(2); gate(0, 0)
            gate(0, 1); high_h(0, 0); gate(0, 2); high_h(0, 1); high_x(1); gate(0, 3); gate(0, 4); high_h(0, 2)
            gate(0, 5); normalise(2); high_h(0, 3); gate(1, 0); high_x(2); high_h(0, 4); gate(1, 1); high_h(0, 5)
            high_h(1, 0); gate(1, 2); last_down_weights(); high_h(1, 1); gate(1, 3); normalise(3); high_h(1, 2)
            high_h(1, 3); gate(1, 4); copy_select(); gate(1, 5); gate(2, 0); high_x(3); high_h(1, 4); gate(2, 1)
            normalise(4); high_h(1, 5); gate(2, 2); high_h(2, 0); attn_x(0); high_h(2, 1); high_h(2, 2); gate(2, 3)
            high_wx2(); high_h(2, 3); gate(2, 4); low_rank_tanh(0); high_z(0); gate(2, 5); high_h(2, 4); gate(3, 0)
            high_h(2, 5); stack_copy(0, 0); high_h(3, 0); normalise(5); gate(3, 1); stack_copy(0, 1); high_h(3, 1)
            stack_copy(0, 2); attn_x(1); values(0); decay_tanh(0); low_rank_tanh(1); high_z(1); gate(3, 2)
            decays(0); stack_copy(1, 0); keys(0); high_h(3, 2); receptance(0); stack_copy(1, 1); normalise(6)
            gate(3, 3); gates(0); attn_x(2); decay_tanh(1); stack_copy(1, 2); high_h(3, 3); gate(3, 4); values(1)
            low_rank_tanh(2); high_z(2); gate(3, 5); high_h(3, 4); high_h(3, 5); stack_copy(2, 0); keys(1)
            stack_copy(2, 1); receptance(1); squares(0); decays(1); stack_copy(2, 2); head_std(0); gates(1)
            decay_tanh(2); values(2); normalise(7); norm_affine(0); attn_x(3); decays(2); keys(2); low_rank_tanh(3)
            high_z(3); receptance(2); stack_copy(3, 0); normalise(8); stack_copy(3, 1); high_x(4); squares(1)
            gates(2); decay_tanh(3); gate(4, 0); head_std(1); values(3); norm_affine(1); high_h(4, 0); gate(4, 1)
            gate(4, 2); decays(3); keys(3); gate(4, 3); high_h(4, 1); normalise(9); stack_copy(3, 2); receptance(3)
            high_h(4, 2); squares(2); gate(4, 4); high_h(4, 3); gate(4, 5); high_x(5); head_std(2); high_h(4, 4)
            norm_affine(2); gate(5, 0); gate(5, 1); high_h(4, 5); squares(3); high_h(5, 0); high_h(5, 1); gate(5, 2)
            head_std(3); gates(3); normalise(10); norm_affine(3); gate(5, 3); gate(5, 4); high_h(5, 2); high_x(6)
            high_h(5, 3); gate(5, 5); high_h(5, 4); gate(6, 0); high_h(5, 5); gate(6, 1); high_h(6, 0); gate(6, 2)
            normalise(11); high_h(6, 1); gate(6, 3); high_x(7); high_h(6, 2); gate(6, 4); high_h(6, 3); gate(6, 5)
            high_h(6, 4); high_h(6, 5); gate(7, 0); gate(7, 1); high_h(7, 0); gate(7, 2); high_h(7, 1); high_h(7, 2)
            gate(7, 3); gate(7, 4); high_h(7, 3); gate(7, 5); high_h(7, 4); high_h(7, 5)

        @block.gpsimd
        def _(pool):
            def constants():
                pool.memset(vrep[:, 1, 0, :, :], 0.0).then_inc(zeros_ready, 1)
                pool.memset(minus_half[:, :], -0.5).then_inc(consts, 1)
                pool.memset(xlt[:, :, 0:1], 0.0)
                pool.memset(state[:, :, 0:1], 0.0).then_inc(consts, 1)
                pool.wait_ge(consts, 2)

            def halve_sdown():
                pool.wait_ge(sdn_in, 16)
                pool.tensor_scalar(sdn[:, :], sdn[:, :], 0.5, None, ALU.mult).then_inc(consts, 1)

            def root(l):
                pool.wait_ge(var_ready, l + 1)
                pool.tensor_tensor(rstd[:, l, :], var_eps[:, l, :], minus_half[:, :], ALU.pow).then_inc(rstd_ready, 1)
                pool.wait_ge(rstd_ready, l + 1)
                pool.wait_ge(mean_ready, l + 1)
                pool.tensor_tensor(norm_bias[:, l, :], minus_mean[:, l, :], rstd[:, l, :], ALU.mult).then_inc(norm_ready, 1)

            def low_h(u, j):
                pool.wait_ge(hhi_ready, FC * u + j + 1)
                if u:
                    pool.wait_ge(down_done, FC * (u - 1) + j + 1)
                pool.tensor_tensor(hlo[:, j, :], hf[:, (FC * u + j) % RING, :], hhi[:, j, :].bitcast(fp32),
                                   ALU.subtract).then_inc(hlo_ready, 1)

            def low_z(h):
                pool.wait_ge(z_hi_ready, h + 1)
                pool.tensor_tensor(z_parts[:, 1, :, :], z[:, :, :], z_parts[:, 0, :, :].bitcast(fp32),
                                   ALU.subtract).then_inc(z_lo_ready, 1)

            def add_ffn(u):
                h = u % NQ
                pool.wait_ge(ffn_out_ready, u + 1)
                rows = xs[:, SUB * h:SUB * (h + 1), :]
                pool.tensor_tensor(rows, rows, ffn_out[:, u % 2, :, :], ALU.add).then_inc(residual_ready, 1)

            def add_x(h, m):
                n = mix_number(h, m)
                pool.wait_ge(scaled_ready, n + 1)
                pool.tensor_tensor(mix[:, n % MRING, :, :], mix[:, n % MRING, :, :],
                                   xlt[:, :, TQ * h + 1:TQ * (h + 1) + 1], ALU.add).then_inc(mix_ready, 1)

            def read_state(h, q):
                pool.wait_ge(scan_ready, HV * h + 2 * q + 2)
                pool.wait_ge(r_ready, h + 1)
                pool.tensor_tensor(vrep[:, h % 2, q, :, :],
                                   rt[:, h % 2, :].unsqueeze(1).to_broadcast([P, 2, TQ]),
                                   state[:, 2 * q:2 * q + 2, TQ * h:TQ * (h + 1)], ALU.mult).then_inc(read_ready[1], 1)

            constants(); root(0); root(1); root(2); low_h(0, 0); low_h(0, 1); low_h(0, 2); halve_sdown()
            low_h(0, 3); low_h(0, 4); low_h(1, 0); root(3); low_h(1, 1); add_ffn(0); low_h(1, 2); low_h(1, 3)
            root(4); low_h(1, 4); low_h(2, 0); low_h(2, 1); add_ffn(1); low_h(2, 2); low_h(2, 3); low_z(0)
            low_h(2, 4); root(5); low_h(3, 0); add_x(0, "w"); add_x(0, "v"); add_ffn(2); add_x(0, "k")
            add_x(0, "r"); low_h(3, 1); low_z(1); add_x(0, "g"); root(6); low_h(3, 2); add_x(1, "w"); add_x(1, "v")
            low_h(3, 3); read_state(0, 1); low_z(2); read_state(0, 3); add_x(1, "k"); add_x(1, "r"); add_x(1, "g")
            low_h(3, 4); add_x(2, "w"); add_x(2, "v"); add_ffn(3); add_x(2, "k"); root(7); read_state(1, 0)
            read_state(1, 2); read_state(1, 3); add_x(2, "r"); low_z(3); root(8); add_x(2, "g"); add_x(3, "w")
            add_x(3, "v"); read_state(2, 0); read_state(2, 2); low_h(4, 0); add_x(3, "k"); add_x(3, "r")
            read_state(2, 3); root(9); low_h(4, 1); read_state(3, 0); low_h(4, 2); read_state(3, 1)
            read_state(3, 2); low_h(4, 3); read_state(3, 3); low_h(4, 4); add_x(3, "g"); low_h(5, 0); root(10)
            low_h(5, 1); low_h(5, 2); low_h(5, 3); low_h(5, 4); root(11); low_h(6, 0); low_h(6, 1); add_ffn(4)
            low_h(6, 2); low_h(6, 3); add_ffn(5); low_h(6, 4); low_h(7, 0); low_h(7, 1); low_h(7, 2); add_ffn(6)
            low_h(7, 3); low_h(7, 4); add_ffn(7)

        @block.sync
        def _(sp):
            def load(dst, src, ready):
                sp.dma_start(dst, src).then_inc(ready, 16)

            xv = x[0, :, :].rearrange("(n p) d -> p n d", p=P)
            wguv = wgu.rearrange("(c p) f -> p c f", p=P)

            def load_x(h):
                load(xs[:, SUB * h:SUB * (h + 1), :], xv[:, SUB * h:SUB * (h + 1), :], x_in[h])

            def load_wgu(q):
                lo, hi = WGU_PARTS[q]
                load(wgu_int[:, :, lo:hi], wguv[:, :, lo:hi], wgu_in[q])

            def load_wd(q):
                lo, hi = WD_PARTS[q]
                load(wd_int[:, lo:hi, :], wd[lo * P:hi * P, :].rearrange("(c p) d -> p c d", p=P), wd_in[q])

            load_x(0)
            load_wgu(0)
            load(idt[:, :], ident, idt_in)
            load_x(1)
            load(tab[:, :], table, tab_in)
            load_wgu(1)
            load_wd(0)
            load_wgu(2)
            load_x(2)
            load_wd(1)
            load(wd_int[P - REM:P, FULL, :], wd[FULL * P:F, :], wd_last_in)
            load(sdn[:, :], sdown.partition_broadcast(P), sdn_in)
            load_x(3)
            load(wx1s[:, :, :], wx1.rearrange("(c p) f -> p c f", p=P), wz_in)
            load(select, selector.rearrange("p (a q) -> p a q", a=6), wz_in)
            for a in range(QUADRANTS):
                load(wx2_raw[a * RLO:(a + 1) * RLO], wx2.rearrange("(m r) d -> r m d", r=RLO), wx2_in)
            for dst, src in ((ww1s, ww1), (wvs, wv), (wks, wk), (wrs, wr), (wgs, wg), (wos, wo)):
                load(dst[:, :, :], src.rearrange("(c p) f -> p c f", p=P), wp_in)
            load(ww2s[:, :], ww2, wp_in)
            load(rept[:, :], rep, wp_in)
            def value_planes(h):
                sp.wait_ge(v_ready, h + 1)
                sp.dma_start(v_dram[h, :, :], vt[:, h % 2, :, :].rearrange("p c t -> p (c t)")).then_inc(v_out[h], 16)
                sp.wait_ge(v_out[h], 16)
                if h >= 2:
                    sp.wait_ge(key_summed, PAIRS * (h - 1))
                for k in range(HQK):
                    sp.dma_start(vrep[k * NH:(k + 1) * NH, h % 2, :, :, :].rearrange("n q c t -> n q (c t)"),
                                 v_dram[h, :, :].rearrange("(q n) t -> n q t", n=NH)).then_inc(vrep_in[h], 16)

            def store(h):
                sp.wait_ge(residual_ready, NQ + h + 1)
                rows = slice(SUB * h, SUB * (h + 1))
                sp.dma_start(out[0, :, :].rearrange("(n p) d -> p n d", p=P)[:, rows, :],
                             xs[:, rows, :]).then_inc(stored, 16)

            value_planes(0); value_planes(1); value_planes(2); value_planes(3); store(0); store(1); store(2)
            store(3)
            sp.wait_ge(stored, 16 * NQ)


def kernel(**inputs):
    import numpy as _np
    import concourse.bacc as _bacc
    from concourse import mybir as _mybir
    from concourse.bass_utils import run_bass_kernel_spmd as _run

    a = {n.replace("L0_attn_", "").replace("L0_ffn_", ""): _np.asarray(v) for n, v in inputs.items()}

    def by_key(w):
        return w.reshape(-1, NH, HQK).transpose(0, 2, 1).reshape(-1, NH * HQK)

    def by_value(w):
        return w.reshape(-1, NH, HV).transpose(0, 2, 1).reshape(-1, NH * HV)

    gate, up = a["wq_gate"].T, a["wq_up"].T
    parts = [w[:, j * P:(j + 1) * P] for j in range(FULL) for w in (gate, up)]
    parts += [gate[:, FULL * P:], up[:, FULL * P:]]

    table = _np.zeros((P, C_ALL), _np.float32)
    table[:, C_SG:C_SG + FULL] = a["s_gate"][:FULL * P].reshape(FULL, P).T
    table[:REM, C_SG + FULL] = a["s_gate"][FULL * P:]
    table[:, C_SU:C_SU + FULL] = a["s_up"][:FULL * P].reshape(FULL, P).T
    table[P - REM:, C_SU + FULL] = a["s_up"][FULL * P:]
    table[:, C_MU:C_MU + 2] = a["mu_x"].reshape(KC, P).T
    table[:, C_BW] = by_key(a["bw"])[0]
    table[:, C_BONUS] = by_key(a["bonus"].reshape(-1))[0]
    table[:, C_GNW:C_GNW + 2] = _np.repeat(a["gn_w"], NH).reshape(KC, P).T
    table[:, C_GNB:C_GNB + 2] = _np.repeat(a["gn_b"], NH).reshape(KC, P).T

    arrays = {
        "x": a["hidden_states"], "wgu": _np.concatenate(parts, 1), "wd": a["wq_down"].T, "table": table,
        "sdown": a["s_down"], "wx1": _np.pad(a["Wx1"], ((0, 0), (0, 2 * ZROWS - MIX * RLO))), "wx2": a["Wx2"].reshape(MIX * RLO, D),
        "wr": by_key(a["Wr"]), "wk": by_key(a["Wk"]), "wv": by_value(a["Wv"]), "wg": by_value(a["Wg"]),
        "ww1": a["Ww1"], "ww2": by_key(a["Ww2"]),
        "wo": a["Wo"].reshape(NH, HV, D).transpose(1, 0, 2).reshape(NH * HV, D),
        "ident": _np.eye(P, dtype=_np.float32),
        "rep": _np.tile(_np.eye(NH, dtype=_np.float32), (4, 4)),
        "selector": _np.concatenate([
            _np.kron(_np.outer(_np.arange(ZROWS // RLO) == j, _np.arange(QUADRANTS) % 2 == part).astype(_np.float32),
                     _np.eye(RLO, dtype=_np.float32)) for j in range(ZROWS // RLO) for part in range(2)], 1),
    }
    nc = _bacc.Bacc("TRN2", target_bir_lowering=False, num_devices=1)
    arrays = {n: _np.ascontiguousarray(v) for n, v in arrays.items()}
    args = [nc.dram_tensor(n, v.shape, _mybir.dt.from_np(v.dtype), kind="ExternalInput").ap()
            for n, v in arrays.items()]
    out = nc.dram_tensor("out", (1, T, D), _mybir.dt.float32, kind="ExternalOutput").ap()
    macaron(nc, *args, out)
    r = _run(nc, [arrays], core_ids=[0])
    return r.results[0]["out"]
```
